# Optimizing a Trainium2 kernel written in Bass

```python
import numpy as np
import jax
import jax.numpy as jnp

def _softmax(x, axis=-1):
    return jax.nn.softmax(x, axis=axis)

def _gelu(x):
    return jax.nn.gelu(x, approximate=True)

def _silu(x):
    return jax.nn.silu(x)

def _sigmoid(x):
    return jax.nn.sigmoid(x)

def _layernorm(x, axis=-1, eps=1e-05):
    m = jnp.mean(x, axis=axis, keepdims=True)
    v = jnp.var(x, axis=axis, keepdims=True)
    return (x - m) / jnp.sqrt(v + eps)

def _scatter_add(tgt, idx, src, axis=0):
    return tgt.at[idx].add(src)

def _segment_sum(src, seg, n):
    return jax.ops.segment_sum(src, seg, n)
kernel_name = 'mk_flamingo_gated_d1_seqx_r4_0e3946'

def setup_inputs(seed: int=0):
    np.random.seed(seed)
    _w = jnp.asarray

    def _rec_inputs():
        import jax
        import jax.numpy as jnp
        _rk = jax.random.key(seed)
        x = -7.109e-05 + 0.9999 * jax.random.normal(jax.random.fold_in(_rk, 1), (4, 512, 512), jnp.float32)
        _lenS = 512 - jax.random.randint(jax.random.fold_in(_rk, 7), (4,), 0, max(1, 512 // 4) + 1, jnp.int32)
        _lenS2 = 512 - jax.random.randint(jax.random.fold_in(_rk, 8), (4,), 0, max(1, 512 // 4) + 1, jnp.int32)
        _ctx_2048P = jax.random.normal(jax.random.fold_in(_rk, 11), (4, 16, 512), jnp.float32)
        _ctx_2048c = jax.random.dirichlet(jax.random.fold_in(_rk, 511), 0.3 * jnp.ones((16,), jnp.float32), (4, 512))
        _ctx_2048t = jnp.einsum('bsk,bkd->bsd', _ctx_2048c, _ctx_2048P)
        _ctx_2048t = _ctx_2048t * jax.lax.rsqrt(jnp.mean(jnp.square(_ctx_2048t)) + 1e-12) * 0.953939
        ctx_2048 = -3.05549e-07 + 0.0199987 * (_ctx_2048t + 0.3 * jax.random.normal(jax.random.fold_in(_rk, 611), (4, 512, 512), jnp.float32))
        _g = jax.random.normal(jax.random.fold_in(_rk, 9001), (2, 1), jnp.float32)
        _g = jnp.sign(_g) * jnp.maximum(jnp.abs(_g), 1.0) + (_g == 0) * 1.0
        g_xattn = _g[0]
        g_ffn = _g[1]
        return (x, ctx_2048, g_xattn, g_ffn)
    x, ctx_2048, g_xattn, g_ffn = _rec_inputs()

    def _L0_xattn_setup():
        import jax, jax.numpy as jnp
        import numpy as np
        FP8_MAX = 448.0
        ACT_EPS = 0.0001
        W_EPS = 1e-06
        BLK = 128

        def quant_dequant_act_1x128(x):
            E, M, K = x.shape
            xb = x.reshape(E, M, K // BLK, BLK)
            amax = jnp.max(jnp.abs(xb), axis=-1, keepdims=True)
            safe = jnp.maximum(amax, ACT_EPS)
            q = (xb * (FP8_MAX / safe)).astype(jnp.float8_e4m3fn)
            return (q.astype(jnp.float32) * (safe / FP8_MAX)).reshape(E, M, K)

        def quant_dequant_weight_128x128(w):
            E, N, K = w.shape
            wb = w.reshape(E, N // BLK, BLK, K // BLK, BLK)
            amax = jnp.max(jnp.abs(wb), axis=(2, 4), keepdims=True)
            safe = jnp.maximum(amax, W_EPS)
            q = (wb * (FP8_MAX / safe)).astype(jnp.float8_e4m3fn)
            return (q.astype(jnp.float32) * (safe / FP8_MAX)).reshape(E, N, K)
        key = jax.random.key(seed)
        kx, kw = jax.random.split(key)
        E, M, K, N = (8, 1024, 512, 512)
        x = jax.random.normal(kx, (E, M, K), dtype=jnp.float32)
        weight = jax.random.normal(kw, (E, N, K), dtype=jnp.float32) * 0.02
        return {'x': x, 'weight': weight}
    _L0_xattn_all = _L0_xattn_setup()
    _L0_xattn_in = {k: v for k, v in _L0_xattn_all.items() if k in ()}
    del _L0_xattn_all

    def _L0_ffn_setup():
        import jax, jax.numpy as jnp
        import numpy as np
        E = 16
        D = 512
        H = 352
        HS = 2 * 352
        TOP_K = 6
        ROUTE_SCALE = 1.0
        key = jax.random.key(seed)
        ks = jax.random.split(key, 16)
        s = 0.02
        return {'x': jax.random.normal(ks[0], (4, 256, D), dtype=jnp.float32), 'gate_w': jax.random.normal(ks[1], (E, D), dtype=jnp.float32) * s, 'gate_b': jax.random.normal(ks[2], (E,), dtype=jnp.float32) * s, 'w1': jax.random.normal(ks[3], (E, H, D), dtype=jnp.float32) * s, 'b1': jax.random.normal(ks[4], (E, H), dtype=jnp.float32) * s, 'w2': jax.random.normal(ks[5], (E, D, H), dtype=jnp.float32) * s, 'b2': jax.random.normal(ks[6], (E, D), dtype=jnp.float32) * s, 'w3': jax.random.normal(ks[7], (E, H, D), dtype=jnp.float32) * s, 'b3': jax.random.normal(ks[8], (E, H), dtype=jnp.float32) * s, 'ws1': jax.random.normal(ks[9], (HS, D), dtype=jnp.float32) * s, 'bs1': jax.random.normal(ks[10], (HS,), dtype=jnp.float32) * s, 'ws2': jax.random.normal(ks[11], (D, HS), dtype=jnp.float32) * s, 'bs2': jax.random.normal(ks[12], (D,), dtype=jnp.float32) * s, 'ws3': jax.random.normal(ks[13], (HS, D), dtype=jnp.float32) * s, 'bs3': jax.random.normal(ks[14], (HS,), dtype=jnp.float32) * s}
    _L0_ffn_all = _L0_ffn_setup()
    _L0_ffn_in = {k: v for k, v in _L0_ffn_all.items() if k in ('gate_w', 'gate_b', 'w1', 'b1', 'w2', 'b2', 'w3', 'b3', 'ws1', 'bs1', 'ws2', 'bs2', 'ws3', 'bs3')}
    del _L0_ffn_all
    return {'x': x, 'ctx_2048': ctx_2048, 'g_xattn': g_xattn, 'g_ffn': g_ffn, 'L0_ffn_gate_w': _L0_ffn_in['gate_w'], 'L0_ffn_gate_b': _L0_ffn_in['gate_b'], 'L0_ffn_w1': _L0_ffn_in['w1'], 'L0_ffn_b1': _L0_ffn_in['b1'], 'L0_ffn_w2': _L0_ffn_in['w2'], 'L0_ffn_b2': _L0_ffn_in['b2'], 'L0_ffn_w3': _L0_ffn_in['w3'], 'L0_ffn_b3': _L0_ffn_in['b3'], 'L0_ffn_ws1': _L0_ffn_in['ws1'], 'L0_ffn_bs1': _L0_ffn_in['bs1'], 'L0_ffn_ws2': _L0_ffn_in['ws2'], 'L0_ffn_bs2': _L0_ffn_in['bs2'], 'L0_ffn_ws3': _L0_ffn_in['ws3'], 'L0_ffn_bs3': _L0_ffn_in['bs3']}

def reference(x, ctx_2048, g_xattn, g_ffn, L0_ffn_gate_w, L0_ffn_gate_b, L0_ffn_w1, L0_ffn_b1, L0_ffn_w2, L0_ffn_b2, L0_ffn_w3, L0_ffn_b3, L0_ffn_ws1, L0_ffn_bs1, L0_ffn_ws2, L0_ffn_bs2, L0_ffn_ws3, L0_ffn_bs3):
    import jax
    import jax.numpy as jnp

    def _L0_xattn_ref(x, weight):
        import jax, jax.numpy as jnp
        import numpy as np
        FP8_MAX = 448.0
        ACT_EPS = 0.0001
        W_EPS = 1e-06
        BLK = 128

        def quant_dequant_act_1x128(x):
            E, M, K = x.shape
            xb = x.reshape(E, M, K // BLK, BLK)
            amax = jnp.max(jnp.abs(xb), axis=-1, keepdims=True)
            safe = jnp.maximum(amax, ACT_EPS)
            q = (xb * (FP8_MAX / safe)).astype(jnp.float8_e4m3fn)
            return (q.astype(jnp.float32) * (safe / FP8_MAX)).reshape(E, M, K)

        def quant_dequant_weight_128x128(w):
            E, N, K = w.shape
            wb = w.reshape(E, N // BLK, BLK, K // BLK, BLK)
            amax = jnp.max(jnp.abs(wb), axis=(2, 4), keepdims=True)
            safe = jnp.maximum(amax, W_EPS)
            q = (wb * (FP8_MAX / safe)).astype(jnp.float8_e4m3fn)
            return (q.astype(jnp.float32) * (safe / FP8_MAX)).reshape(E, N, K)
        xq = quant_dequant_act_1x128(x)
        wq = quant_dequant_weight_128x128(weight)
        return jnp.einsum('emk,enk->emn', xq, wq)

    def _L0_ffn_ref(x, gate_w, gate_b, w1, b1, w2, b2, w3, b3, ws1, bs1, ws2, bs2, ws3, bs3):
        import jax, jax.numpy as jnp
        import numpy as np
        E = 16
        D = 512
        H = 352
        HS = 2 * 352
        TOP_K = 6
        ROUTE_SCALE = 1.0
        shape = x.shape
        xf = x.reshape(-1, shape[-1])
        scores = xf @ gate_w.T
        probs = jax.nn.softmax(scores.astype(jnp.float32), axis=-1)
        biased = probs + gate_b
        _, idx = jax.lax.top_k(biased, TOP_K)
        weights = jnp.take_along_axis(probs, idx, axis=1) * ROUTE_SCALE
        weights = weights.astype(x.dtype)
        onehot = jax.nn.one_hot(idx, E, dtype=weights.dtype)
        cw = jnp.einsum('tk,tke->te', weights, onehot)

        def expert_step(y, params):
            W1, B1, W2, B2, W3, B3, c = params
            h = jax.nn.silu(xf @ W1.T + B1) * (xf @ W3.T + B3)
            out = h @ W2.T + B2
            return (y + c[:, None] * out, None)
        y0 = jnp.zeros_like(xf)
        y, _ = jax.lax.scan(expert_step, y0, (w1, b1, w2, b2, w3, b3, cw.T))
        z = jax.nn.silu(xf @ ws1.T + bs1) * (xf @ ws3.T + bs3) @ ws2.T + bs2
        return (y + z).reshape(shape)
    x = x + jnp.tanh(g_xattn[0]) * _L0_xattn_ref(_layernorm(x, axis=-1), ctx_2048)
    x = x + jnp.tanh(g_ffn[0]) * _L0_ffn_ref(_layernorm(x, axis=-1), L0_ffn_gate_w, L0_ffn_gate_b, L0_ffn_w1, L0_ffn_b1, L0_ffn_w2, L0_ffn_b2, L0_ffn_w3, L0_ffn_b3, L0_ffn_ws1, L0_ffn_bs1, L0_ffn_ws2, L0_ffn_bs2, L0_ffn_ws3, L0_ffn_bs3)
    return x

_drawn_inputs = setup_inputs


def setup_inputs(seed=0):
    import zlib

    import numpy as np

    out = dict(_drawn_inputs(seed))
    spreads = {}
    factors = {'L0_ffn_gate_w': 7.621,
     'L0_ffn_gate_b': 8.0,
     'L0_ffn_w1': 6.676,
     'L0_ffn_b1': 35.429,
     'L0_ffn_w2': 6.458,
     'L0_ffn_b2': 176.57,
     'L0_ffn_w3': 6.456,
     'L0_ffn_b3': 35.292,
     'L0_ffn_bs1': 64.0,
     'L0_ffn_bs2': 130.13,
     'L0_ffn_bs3': 64.0,
     'L0_ffn_ws1': 8.0,
     'L0_ffn_ws2': 8.0,
     'L0_ffn_ws3': 8.0}
    for name, (base, spread) in spreads.items():
        noise = np.random.default_rng([zlib.crc32(name.encode()), seed]).standard_normal(out[name].shape)
        drawn = base * np.exp(spread * noise) if base else spread * noise
        out[name] = jnp.asarray(drawn.astype(out[name].dtype))
    for name, factor in factors.items():
        out[name] = (out[name] * factor).astype(out[name].dtype)
    return out
```

```python
from contextlib import ExitStack

import concourse.bass as bass
from concourse import mybir

F32 = mybir.dt.float32
F32R = mybir.dt.float32r
I32 = mybir.dt.int32
ALU = mybir.AluOpType
ACT = mybir.ActivationFunctionType
AX = mybir.AxisListType

P = 128
NB = 4
BT = 512
NT = BT // P
T = NB * BT
D = 512
KC = D // P
E = 16
TOP_K = 6
H = 352
HS = 704
HID = E * H + HS
CH = -(-HID // P)
W = 3 * D + 2
UNIT = 32
UPC = P // UNIT
UNITS = CH * UPC
UE = H // UNIT
STEPS = CH * NB
BODY = 2 * NB
LOOPS = (STEPS - 2) // BODY
FP8_MAX = 448.0
ACT_EPS = 1e-4
W_EPS = 1e-6
LN_EPS = 1e-5
EXP_MASK = 0x7F800000
FP8_LEAST = 2.0 ** -6
FP8_ROUND = 1.5 * 2.0 ** 20
ABSENT = -1e30
TAKEN = -3e38
T_USES = 2 * NT + 1
SC = 4
GCH = 8 + 2 * NT
X_USES = 2 * NT + 1


def build(nc, t):
    assert H % UNIT == 0 and HS % UNIT == 0 and CH % 2 == 0
    with ExitStack() as ctx:
        def sb(name, shape, dt=F32):
            return ctx.enter_context(nc.sbuf_tensor(name + "_sb", shape, dt))

        def sem(name):
            return ctx.enter_context(nc.semaphore(name))

        xT_hi = sb("xT_hi", [P, KC, T], F32R)
        xT_lo = sb("xT_lo", [P, KC, T], F32R)
        y = sb("y", [P, T // P, D])
        ident = sb("ident", [P, P])
        bias_o = sb("bias_o", [E + 1, D])
        gate_raw = sb("gate_raw", [P, KC, E])
        gate_hi = sb("gate_hi", [P, KC, P], F32R)
        gate_lo = sb("gate_lo", [P, KC, P], F32R)
        gate_bias = sb("gate_bias", [P, E])
        tanh_g = sb("tanh_g", [P, 2])
        const_half = sb("const_half", [P, NT])

        bias_h = sb("bias_h", [P, 2, 2])
        w_raw = sb("w_raw", [P, W])
        w_hi = [sb(f"w_hi{j}", [P, 3 * D], F32R) for j in range(2)]
        w_lo = [sb(f"w_lo{j}", [P, 3 * D], F32R) for j in range(2)]
        c_bc = sb("c_bc", [P, NB, BT])
        sh = sb("silu_h32", [P, 4, BT])
        silu, h32 = sh[:, 0:2, :], sh[:, 2:4, :]
        h_hi = [sb(f"h_hi{j}", [P, BT], F32R) for j in range(2)]
        h_lo = [sb(f"h_lo{j}", [P, BT], F32R) for j in range(2)]

        ctx_v = sb("ctx_v", [P, KC * D])
        ctx_m = c_bc[:].rearrange("p b n -> p (b n)")
        ctx_hi = sb("ctx_hi", [P, KC, D], F32R)
        ctx_lo = sb("ctx_lo", [P, KC, D], F32R)
        ctx_s = sb("ctx_s", [P, 4, 16])
        xa = sb("xa", [P, NT, D])
        xm = sh
        xs = sb("xs", [P, 4, 16])
        a_hi = [sb(f"a_hi{j}", [P, KC, P], F32R) for j in range(2)]
        a_lo = [sb(f"a_lo{j}", [P, KC, P], F32R) for j in range(2)]
        stat = sb("stat", [P, NT, 6])
        mv = sb("mv", [P, NT, 2])
        rs = sb("rs", [P, 4, NT])
        score = sb("score", [E, BT])
        gt = sb("gt", [P, 3, NT, E])
        biased = sb("biased", [P, 2, NT, E + 2])
        top8 = sb("top8", [P, NT, 8])
        g1 = sb("g1", [P, 3, NT])
        cw = sb("cw", [P, NT, E + 1])
        cwT = sb("cwT", [E + 1, BT])

        cexp = nc.dram_tensor("cexp", [UNITS, T], F32).ap()

        bank = [ctx.enter_context(nc.psum_tensor(f"bank{i}", [P, 512], F32)) for i in range(8)]
        psA, psB, psY = bank[0:2], bank[2:4], bank[4:6]
        psT, psX = bank[6], bank[7]

        S = {}
        for n in ("gates_in", "x_in", "ctx_in", "set_up", "tanh_done", "gate_hi_done", "gate_lo_done",
                  "cmax", "call", "cscale", "cv", "cm", "cq", "chi", "clo",
                  "st", "aggr", "powd", "rstd", "xn", "amax", "xsc", "xv", "xmg", "xq", "xdq",
                  "tp", "t_hi", "psT_free", "xmm", "psX_free", "gmm", "gtp", "gch", "gexp", "cwd",
                  "cwtp", "cstored", "bmm",
                  "w_in", "w_hi_done", "w_lo_done", "a_ready", "b_ready", "silu_done",
                  "sc_done", "h_done", "hi_done", "lo_done", "y_ready", "y_free", "stored"):
            S[n] = sem(n)
        SEED, SEEDED = 1, ("tp", "xmm", "gtp", "cwtp", "psT_free", "psX_free")
        c_in = [sem(f"c_in{b}") for b in range(NB)]

        block = ctx.enter_context(nc.Block())

        def val(k, o, per=1, extra=0):
            return k * (BODY * per) + (o * per + extra)

        @block.sync
        def _(sp):
            sp.sem_inc(S["cstored"], 16 * SEED)
            sp.dma_start(y[:, 0:NT, :], t["x"][0:BT].rearrange("(n p) d -> p n d", p=P)).then_inc(S["x_in"], 16)
            sp.dma_start(ctx_v[:].rearrange("p (c n) -> p c n", c=KC),
                         t["ctxT"][0].rearrange("(c p) n -> p c n", p=P)).then_inc(S["ctx_in"], 16)
            sp.dma_start(ident[:], t["ident"]).then_inc(S["gates_in"], 16)
            sp.dma_start(gate_raw[:], t["gate_wT"].rearrange("(c p) e -> p c e", p=P)).then_inc(S["gates_in"], 16)
            sp.dma_start(tanh_g[:, 0:1], t["g_xattn"].partition_broadcast(P)).then_inc(S["gates_in"], 16)
            sp.dma_start(tanh_g[:, 1:2], t["g_ffn"].partition_broadcast(P)).then_inc(S["gates_in"], 16)
            sp.dma_start(gate_bias[:], t["gate_b"].partition_broadcast(P)).then_inc(S["gates_in"], 16)
            sp.dma_start(bias_o[:], t["bias_o"]).then_inc(S["gates_in"], 16)
            sp.dma_start(w_raw[:], t["w_all"][0]).then_inc(S["w_in"], 16)
            x_t = t["x"].rearrange("(b n p) d -> b p n d", p=P, n=NT)
            ctx_t = t["ctxT"].rearrange("b (c p) n -> b p c n", p=P)
            ctx_dst = ctx_v[:].rearrange("p (c n) -> p c n", c=KC)

            def spread_c(b):
                sp.wait_ge(S["psT_free"], SEED + T_USES * (b + 1))
                cols = bass.ds(b * BT, BT)
                sp.dma_start(cexp[0:E * UE, cols].rearrange("(e u) n -> e u n", u=UE),
                             cwT[0:E, :].unsqueeze(1).broadcast_to([E, UE, BT])).then_inc(S["cstored"], 16)
                sp.dma_start(cexp[E * UE:UNITS, cols].rearrange("(e u) n -> e u n", e=1),
                             cwT[E:E + 1, :].unsqueeze(1).broadcast_to([1, UNITS - E * UE, BT])
                             ).then_inc(S["cstored"], 16)

            with sp.Fori(0, NB - 1) as b:
                sp.wait_ge(S["x_in"], 16 * (b + 1))
                sp.dma_start(y[:, bass.ds((b + 1) * NT, NT), :], x_t[bass.ds(b + 1, 1)].squeeze(0)
                             ).then_inc(S["x_in"], 16)
                sp.wait_ge(S["clo"], b + 1)
                sp.dma_start(ctx_dst, ctx_t[bass.ds(b + 1, 1)].squeeze(0)).then_inc(S["ctx_in"], 16)
                spread_c(b)
            spread_c(NB - 1)
            sp.wait_ge(S["cstored"], 16 * SEED + 32 * NB)

            def load_c(g, b):
                src = cexp[bass.ds(g * UPC, UPC), b * BT:(b + 1) * BT]
                sp.dma_start(c_bc[:, b, :], src.unsqueeze(1).broadcast_to([UPC, UNIT, BT])
                             ).then_inc(c_in[b], 16)

            for b in range(NB):
                load_c(0, b)

            def step(k, o):
                b, g = o % NB, k * 2 + o // NB
                sp.wait_ge(S["sc_done"], val(k, o, 1, 1))
                load_c(g + 1, b)
                if b == 2:
                    sp.wait_ge(S["w_lo_done"], g + 2)
                    sp.dma_start(w_raw[:], t["w_all"][bass.ds(g + 2, 1)].squeeze(0)).then_inc(S["w_in"], 16)

            sp.wait_ge(S["w_lo_done"], 1)
            sp.dma_start(w_raw[:], t["w_all"][1]).then_inc(S["w_in"], 16)
            step(0, 0)
            step(0, 1)
            with sp.Fori(0, LOOPS) as k:
                for o in range(2, BODY + 2):
                    step(k, o)
            for o in range(BODY * LOOPS + 2, STEPS - NB):
                sp.wait_ge(S["sc_done"], o + 1)
                load_c(o // NB + 1, o % NB)
            out_t = t["out"].rearrange("(b n p) d -> b p n d", p=P, n=NT)
            for b in range(NB):
                sp.wait_ge(S["y_free"], 2 + NT * (STEPS - NB + b + 1))
                sp.dma_start(out_t[b], y[:, b * NT:(b + 1) * NT, :]).then_inc(S["stored"], 16)
            sp.wait_ge(S["stored"], 16 * NB)

        def wait_apart(e, name, value):
            register = e.to_reg(value)
            e.wait_ge(S["set_up"], 4)
            e.wait_ge(S[name], register)

        def prep(e, name, b, n, per):
            e.wait_ge(S[name], b * per + n + (SEED if name in SEEDED else 0))

        @block.gpsimd
        def _(pool):
            pool.memset(const_half[:], -0.5).then_inc(S["set_up"], 1)
            pool.memset(biased[:], ABSENT).then_inc(S["set_up"], 1)
            pool.memset(gate_hi[:].bitcast(F32), 0.0).then_inc(S["set_up"], 1)
            pool.memset(gate_lo[:].bitcast(F32), 0.0).then_inc(S["set_up"], 1)
            pool.wait_ge(S["set_up"], 4)

            def power(b, half):
                wait_apart(pool, "aggr", b * (2 * NT) + NT * (half + 1))
                pool.tensor_scalar(rs[:, 0, :], mv[:, :, 1], LN_EPS, None, ALU.add).then_inc(S["powd"], 1)
                pool.wait_ge(S["powd"], b * 4 + 2 * half + 1)
                pool.tensor_tensor(rs[:, 1, :], rs[:, 0, :], const_half[:], ALU.pow).then_inc(S["powd"], 1)

            cv16 = ctx_v[:].rearrange("p (q n) -> p q n", n=P)
            with pool.Fori(0, NB) as b:
                wait_apart(pool, "cmax", b * (1) + 1)
                pool.partition_all_reduce(ctx_s[:, 1, :], ctx_s[:, 0, :], P, bass.bass_isa.ReduceOp.max
                                          ).then_inc(S["call"], 1)
                power(b, 0)
                prep(pool, "cscale", b, SC, SC)
                pool.tensor_tensor(cv16, cv16, ctx_s[:, 2, :].unsqueeze(2).broadcast_to([P, 16, P]), ALU.mult
                                   ).then_inc(S["cv"], 1)
                prep(pool, "cm", b, 2, 2)
                pool.tensor_tensor(ctx_v[:], ctx_v[:], ctx_m[:], ALU.add).then_inc(S["cq"], 1)
                prep(pool, "cq", b, 1, 3)
                pool.tensor_tensor(ctx_v[:], ctx_v[:], ctx_m[:], ALU.subtract).then_inc(S["cq"], 1)
                prep(pool, "cq", b, 2, 3)
                pool.tensor_tensor(cv16, cv16, ctx_s[:, 3, :].unsqueeze(2).broadcast_to([P, 16, P]), ALU.mult
                                   ).then_inc(S["cq"], 1)
                prep(pool, "xmg", b, 2, 2)
                for i in range(NT):
                    pool.tensor_tensor(xa[:, i, :], xa[:, i, :], xm[:, i, :], ALU.add).then_inc(S["xq"], 1)
                for i in range(NT):
                    prep(pool, "xq", b, i + 1, 2 * NT)
                    pool.tensor_tensor(xa[:, i, :], xa[:, i, :], xm[:, i, :], ALU.subtract).then_inc(S["xq"], 1)
                power(b, 1)

            def split_lo(g, j):
                pool.wait_ge(S["w_hi_done"], 2 * g + 2)
                pool.tensor_tensor(w_lo[j][:], w_raw[:, 0:3 * D], w_hi[j][:].bitcast(F32), ALU.subtract
                                   ).then_inc(S["w_lo_done"], 1)

            def step(k, o, last=False):
                b, j = o % NB, o % 2
                pool.wait_ge(S["silu_done"], val(k, o, 1, 1))
                pool.wait_ge(c_in[b], (k * 2 + o // NB + 1) * 16)
                pool.tensor_tensor(silu[:, j, :], silu[:, j, :], c_bc[:, b, :], ALU.mult).then_inc(S["sc_done"], 1)
                if b == 2 and not last:
                    split_lo(k * 2 + o // NB + 1, (o // NB + 1) % 2)

            split_lo(0, 0)
            step(0, 0)
            step(0, 1)
            with pool.Fori(0, LOOPS) as k:
                for o in range(2, BODY + 2):
                    step(k, o)
            for o in range(BODY * LOOPS + 2, STEPS):
                step(0, o, last=o >= STEPS - NB)

        @block.scalar
        def _(act):
            def copy(out, in_):
                return nc.scalar.activation(out, in_, ACT.Copy)

            def split_hi(j):
                copy(bias_h[:, j, :], w_raw[:, 3 * D:W]).then_inc(S["w_hi_done"], 1)
                copy(w_hi[j][:], w_raw[:, 0:3 * D]).then_inc(S["w_hi_done"], 1)

            act.wait_ge(S["gates_in"], 16 * 6)
            nc.scalar.activation(tanh_g[:], tanh_g[:], ACT.Tanh).then_inc(S["tanh_done"], 1)
            act.wait_ge(S["set_up"], 4)
            copy(gate_hi[:, :, 0:E], gate_raw[:]).then_inc(S["gate_hi_done"], 1)
            act.wait_ge(S["w_in"], 16)
            split_hi(0)
            with act.Fori(0, NB) as b:
                prep(act, "cq", b, 3, 3)
                act.wait_ge(S["xmm"], SEED + b * NT)
                copy(ctx_hi[:].rearrange("p c n -> p (c n)"), ctx_v[:]).then_inc(S["chi"], 1)
                for i in range(NT):
                    prep(act, "tp", b, i + 1, 2 * NT)
                    act.wait_ge(S["xmm"], SEED + b * NT + max(i - 1, 0))
                    copy(a_hi[i % 2][:].rearrange("p c n -> p (c n)"), psT[:]).then_inc(S["t_hi"], 1)
                for i in range(NT):
                    prep(act, "tp", b, NT + i + 1, 2 * NT)
                    copy(xT_hi[:, :, bass.ds(b * BT + i * P, P)], psT[:].rearrange("p (c n) -> p c n", c=KC)
                         ).then_inc(S["t_hi"], 1)
                prep(act, "gmm", b, 1, 1)
                act.wait_ge(S["gtp"], SEED + b)
                copy(score[:], psX[0:E, :]).then_inc(S["psX_free"], 1)
                prep(act, "gch", b, 2, GCH)
                nc.scalar.activation(gt[:, 1], gt[:, 0], ACT.Exp).then_inc(S["gexp"], 1)
                prep(act, "cwtp", b, 1, 1)
                act.wait_ge(S["cstored"], 16 * SEED + b * 32)
                act.wait_ge(S["psX_free"], SEED + b * X_USES)
                copy(cwT[:], psT[0:E + 1, :]).then_inc(S["psT_free"], 1)

            def step(k, o, last=False):
                b, j = o % NB, o % 2
                g = k * 2 + o // NB
                act.wait_ge(S["a_ready"], val(k, o, 1, 1))
                if o > 1:
                    act.wait_ge(S["h_done"], val(k, o, 1, -1))
                nc.scalar.activation(silu[:, j, :], psA[j][:], ACT.Silu, bias=bias_h[:, (o // NB) % 2, 0:1]
                                     ).then_inc(S["silu_done"], 1)
                if b == 1 and not last:
                    act.wait_ge(S["w_in"], g * 16 + 32)
                    if o > 1:
                        act.wait_ge(S["y_ready"], g * (NB * NT))
                    split_hi((o // NB + 1) % 2)
                act.wait_ge(S["h_done"], val(k, o, 1, 1))
                if o > 1:
                    act.wait_ge(S["y_ready"], val(k, o, NT, -NT))
                copy(h_hi[j][:], h32[:, j, :]).then_inc(S["hi_done"], 1)

            step(0, 0)
            step(0, 1)
            with act.Fori(0, LOOPS) as k:
                for o in range(2, BODY + 2):
                    step(k, o)
            for o in range(BODY * LOOPS + 2, STEPS):
                step(0, o, last=o >= STEPS - NB)

        @block.vector
        def _(dve):
            V = nc.vector
            for n in SEEDED:
                dve.sem_inc(S[n], SEED)
            dve.wait_ge(S["set_up"], 4)
            dve.wait_ge(S["gate_hi_done"], 1)
            V.tensor_tensor(gate_lo[:, :, 0:E], gate_raw[:], gate_hi[:, :, 0:E].bitcast(F32), ALU.subtract
                            ).then_inc(S["gate_lo_done"], 1)
            dve.wait_ge(S["tanh_done"], 1)
            V.tensor_copy(cw[:, :, E:E + 1], tanh_g[:, 1:2].unsqueeze(1).broadcast_to([P, NT, 1])
                          ).then_inc(S["gate_lo_done"], 1)

            def statistics(b, half):
                for i in range(NT):
                    if half:
                        wait_apart(dve, "psX_free", SEED + b * X_USES + i + 1)
                    V.bn_stats(stat[:, i, :], y[:, bass.ds(b * NT + i, 1), :].squeeze(1)).then_inc(S["st"], 1)
                for i in range(NT):
                    wait_apart(dve, "st", b * (2 * NT) + half * NT + i + 1)
                    V.bn_aggr(mv[:, i, :], stat[:, i, :]).then_inc(S["aggr"], 1)

            def normalise(b, half):
                prep(dve, "powd", b, 2 * half + 2, 4)
                V.tensor_tensor(rs[:, 2, :], rs[:, 1, :], rs[:, 1, :], ALU.mult).then_inc(S["rstd"], 1)
                prep(dve, "rstd", b, 4 * half + 1, 8)
                V.tensor_tensor(rs[:, 2, :], rs[:, 2, :], rs[:, 0, :], ALU.mult).then_inc(S["rstd"], 1)
                prep(dve, "rstd", b, 4 * half + 2, 8)
                V.tensor_scalar(rs[:, 2, :], rs[:, 2, :], -0.5, 1.5, ALU.mult, ALU.add).then_inc(S["rstd"], 1)
                prep(dve, "rstd", b, 4 * half + 3, 8)
                V.tensor_tensor(rs[:, 3, :], rs[:, 1, :], rs[:, 2, :], ALU.mult).then_inc(S["rstd"], 1)
                prep(dve, "rstd", b, 4 * half + 4, 8)
                dve.wait_ge(S["tp"], SEED + b * (2 * NT) + half * NT)
                for i in range(NT):
                    V.tensor_scalar(xa[:, i, :], y[:, bass.ds(b * NT + i, 1), :].squeeze(1), mv[:, i, 0:1],
                                    rs[:, 3, i:i + 1], ALU.subtract, ALU.mult).then_inc(S["xn"], 1)

            def scales(s, name, b):
                prep(dve, name, b, 1, SC)
                V.reciprocal(s[:, 2, :], s[:, 1, :]).then_inc(S[name], 1)
                V.tensor_scalar(s[:, 3, :], s[:, 1, :], 1.0 / FP8_MAX, None, ALU.mult).then_inc(S[name], 1)
                prep(dve, name, b, 2, SC)
                V.tensor_scalar(s[:, 2, :], s[:, 2, :], FP8_MAX, None, ALU.mult).then_inc(S[name], 1)
                prep(dve, name, b, SC, SC)

            def magic(v, m, name, b):
                V.tensor_scalar(m[:].bitcast(I32), v[:].bitcast(I32), EXP_MASK, None, ALU.bitwise_and
                                ).then_inc(S[name], 1)
                prep(dve, name, b, 1, 2)
                V.tensor_scalar(m[:], m[:], FP8_LEAST, FP8_ROUND, ALU.max, ALU.mult).then_inc(S[name], 1)

            xa16 = xa[:].rearrange("p i (c n) -> p (i c) n", n=P)
            cv16 = ctx_v[:].rearrange("p (q n) -> p q n", n=P)
            with dve.Fori(0, NB) as b:
                dve.wait_ge(S["ctx_in"], (b + 1) * 16)
                V.tensor_reduce(ctx_s[:, 0, :], cv16, AX.X, ALU.max, apply_absolute_value=True
                                ).then_inc(S["cmax"], 1)
                dve.wait_ge(S["x_in"], (b + 1) * 16)
                statistics(b, 0)
                prep(dve, "call", b, 1, 1)
                V.tensor_scalar(ctx_s[:, 1, :], ctx_s[:, 1, :], W_EPS, None, ALU.max).then_inc(S["cscale"], 1)
                scales(ctx_s, "cscale", b)
                normalise(b, 0)
                prep(dve, "xn", b, NT, 2 * NT)
                V.tensor_reduce(xs[:, 0, :], xa16, AX.X, ALU.max, apply_absolute_value=True).then_inc(S["amax"], 1)
                prep(dve, "amax", b, 1, 1)
                V.tensor_scalar(xs[:, 1, :], xs[:, 0, :], ACT_EPS, None, ALU.max).then_inc(S["xsc"], 1)
                scales(xs, "xsc", b)
                V.tensor_tensor(xa16, xa16, xs[:, 2, :].unsqueeze(2).broadcast_to([P, 16, P]), ALU.mult
                                ).then_inc(S["xv"], 1)
                prep(dve, "xv", b, 1, 1)
                magic(xa, xm, "xmg", b)
                prep(dve, "cv", b, 1, 1)
                magic(ctx_v, ctx_m, "cm", b)
                for i in range(NT):
                    prep(dve, "xq", b, NT + i + 1, 2 * NT)
                    xt = xa[:, i, :].rearrange("p (c n) -> p c n", n=P)
                    V.tensor_tensor(xt, xt, xs[:, 3, i * KC:(i + 1) * KC].unsqueeze(2).broadcast_to([P, KC, P]),
                                    ALU.mult).then_inc(S["xdq"], 1)
                prep(dve, "chi", b, 1, 1)
                V.tensor_tensor(ctx_lo[:].rearrange("p c n -> p (c n)"), ctx_v[:],
                                ctx_hi[:].rearrange("p c n -> p (c n)").bitcast(F32), ALU.subtract
                                ).then_inc(S["clo"], 1)

                def residual(i):
                    prep(dve, "xmm", b, i + 1, NT)
                    yt = y[:, bass.ds(b * NT + i, 1), :].squeeze(1)
                    V.scalar_tensor_tensor(yt, psX[:], tanh_g[:, 0:1], yt, ALU.mult, ALU.add
                                           ).then_inc(S["psX_free"], 1)

                for i in range(NT):
                    prep(dve, "t_hi", b, i + 1, 2 * NT)
                    dve.wait_ge(S["xmm"], SEED + b * NT + max(i - 1, 0))
                    V.tensor_tensor(a_lo[i % 2][:].rearrange("p c n -> p (c n)"), psT[:],
                                    a_hi[i % 2][:].rearrange("p c n -> p (c n)").bitcast(F32), ALU.subtract
                                    ).then_inc(S["psT_free"], 1)
                    if i:
                        residual(i - 1)
                residual(NT - 1)
                statistics(b, 1)
                normalise(b, 1)
                for i in range(NT):
                    prep(dve, "t_hi", b, NT + i + 1, 2 * NT)
                    cols = bass.ds(b * BT + i * P, P)
                    V.tensor_tensor(xT_lo[:, :, cols], psT[:].rearrange("p (c n) -> p c n", c=KC),
                                    xT_hi[:, :, cols].bitcast(F32), ALU.subtract).then_inc(S["psT_free"], 1)
                prep(dve, "gtp", b, 1, 1)
                ps = psT[:, 0:NT * E].rearrange("p (i e) -> p i e", e=E)
                V.tensor_reduce(g1[:, 0, :], ps, AX.X, ALU.max).then_inc(S["gch"], 1)
                prep(dve, "gch", b, 1, GCH)
                V.tensor_tensor(gt[:, 0], ps, g1[:, 0, :].unsqueeze(2).broadcast_to([P, NT, E]), ALU.subtract
                                ).then_inc(S["gch"], 1)
                prep(dve, "gexp", b, 1, 1)
                V.tensor_reduce(g1[:, 1, :], gt[:, 1], AX.X, ALU.add).then_inc(S["gch"], 1)
                prep(dve, "gch", b, 3, GCH)
                V.reciprocal(g1[:, 2, :], g1[:, 1, :]).then_inc(S["gch"], 1)
                prep(dve, "gch", b, 4, GCH)
                V.tensor_tensor(gt[:, 2], gt[:, 1], g1[:, 2, :].unsqueeze(2).broadcast_to([P, NT, E]), ALU.mult
                                ).then_inc(S["gch"], 1)
                prep(dve, "gch", b, 5, GCH)
                V.tensor_tensor(biased[:, 0, :, 0:E], gt[:, 2], gate_bias[:].unsqueeze(1).broadcast_to([P, NT, E]),
                                ALU.add).then_inc(S["gch"], 1)
                wait_apart(dve, "gch", b * GCH + 6)
                for i in range(NT):
                    V.max(top8[:, i, :], biased[:, 0, i, 0:E]).then_inc(S["gch"], 1)
                prep(dve, "gch", b, 6 + NT, GCH)
                V.memset(top8[:, :, TOP_K:8], ABSENT).then_inc(S["gch"], 1)
                wait_apart(dve, "gch", b * GCH + 7 + NT)
                for i in range(NT):
                    V.match_replace(biased[:, 1, i, :], top8[:, i, :], biased[:, 0, i, :], TAKEN
                                    ).then_inc(S["gch"], 1)
                prep(dve, "gch", b, 7 + 2 * NT, GCH)
                V.scalar_tensor_tensor(gt[:, 0], biased[:, 1, :, 0:E], TAKEN, gt[:, 2], ALU.is_equal, ALU.mult
                                       ).then_inc(S["gch"], 1)
                prep(dve, "gch", b, 8 + 2 * NT, GCH)
                dve.wait_ge(S["cwtp"], SEED + b)
                V.tensor_scalar(cw[:, :, 0:E], gt[:, 0], tanh_g[:, 1:2], None, ALU.mult).then_inc(S["cwd"], 1)
                for i in range(NT):
                    prep(dve, "bmm", b, i + 1, NT)
                    yt = y[:, bass.ds(b * NT + i, 1), :].squeeze(1)
                    V.tensor_tensor(yt, psX[:], yt, ALU.add).then_inc(S["psX_free"], 1)
            dve.wait_ge(S["psX_free"], SEED + X_USES * NB)
            dve.nop().then_inc(S["y_free"], 2)

            def add_out(k, o, i):
                dve.wait_ge(S["y_ready"], val(k, o, NT, -NT + i + 1))
                q = ((o - 1) % NB) * NT + i
                V.tensor_tensor(y[:, q, :], psY[i % 2][:], y[:, q, :], ALU.add).then_inc(S["y_free"], 1)

            def step(k, o):
                j = o % 2
                if o > 0:
                    add_out(k, o, 0)
                    add_out(k, o, 1)
                dve.wait_ge(S["b_ready"], val(k, o, 1, 1))
                dve.wait_ge(S["sc_done"], val(k, o, 1, 1))
                if o > 1:
                    dve.wait_ge(S["lo_done"], val(k, o, 1, -1))
                V.scalar_tensor_tensor(h32[:, j, :], psB[j][:], bias_h[:, (o // NB) % 2, 1:2],
                                       silu[:, j, :], ALU.add, ALU.mult).then_inc(S["h_done"], 1)
                if o > 0:
                    add_out(k, o, 2)
                dve.wait_ge(S["hi_done"], val(k, o, 1, 1))
                V.tensor_tensor(h_lo[j][:], h32[:, j, :], h_hi[j][:].bitcast(F32), ALU.subtract
                                ).then_inc(S["lo_done"], 1)
                if o > 0:
                    add_out(k, o, 3)

            step(0, 0)
            step(0, 1)
            with dve.Fori(0, LOOPS) as k:
                for o in range(2, BODY + 2):
                    step(k, o)
            for o in range(BODY * LOOPS + 2, STEPS):
                step(0, o)
            for i in range(NT):
                add_out(0, STEPS, i)

        @block.tensor
        def _(pe):
            def three(out, a_hi, a_lo, b_hi, b_lo, start, stop):
                nc.tensor.matmul(out, a_hi, b_hi, start=start, stop=False)
                nc.tensor.matmul(out, a_hi, b_lo, start=False, stop=False)
                return nc.tensor.matmul(out, a_lo, b_hi, start=False, stop=stop)

            pe.wait_ge(S["gates_in"], 16 * 6)
            pe.wait_ge(S["gate_lo_done"], 2)
            with pe.Fori(0, NB) as b:
                def transposes(i, half):
                    prep(pe, "xn" if half else "xdq", b, i + 1 + (NT if half else 0), 2 * NT if half else NT)
                    pe.wait_ge(S["psT_free"], SEED + b * T_USES + half * NT + i)
                    for c in range(KC):
                        last = nc.tensor.transpose(psT[:, c * P:(c + 1) * P], xa[:, i, c * P:(c + 1) * P], ident[:])
                    last.then_inc(S["tp"], 1)

                def attend(i):
                    prep(pe, "psT_free", b, i + 1, T_USES)
                    prep(pe, "clo", b, 1, 1)
                    pe.wait_ge(S["psX_free"], SEED + b * X_USES + i)
                    for c in range(KC):
                        last = three(psX[:], a_hi[i % 2][:, c, :], a_lo[i % 2][:, c, :], ctx_hi[:, c, :],
                                     ctx_lo[:, c, :], c == 0, c == KC - 1)
                    last.then_inc(S["xmm"], 1)

                for i in range(NT):
                    transposes(i, 0)
                    if i:
                        attend(i - 1)
                attend(NT - 1)
                for i in range(NT):
                    transposes(i, 1)
                pe.wait_ge(S["psT_free"], SEED + b * T_USES + 2 * NT)
                pe.wait_ge(S["psX_free"], SEED + b * X_USES + NT)
                cols = bass.ds(b * BT, BT)
                for c in range(KC):
                    last = three(psX[:], gate_hi[:, c, :], gate_lo[:, c, :], xT_hi[:, c, cols], xT_lo[:, c, cols],
                                 c == 0, c == KC - 1)
                last.then_inc(S["gmm"], 1)
                wait_apart(pe, "psX_free", SEED + b * X_USES + NT + 1)
                for i in range(NT):
                    last = nc.tensor.transpose(psT[:, i * E:(i + 1) * E], score[:, i * P:(i + 1) * P],
                                               ident[0:E, 0:E])
                last.then_inc(S["gtp"], 1)
                prep(pe, "cwd", b, 1, 1)
                for i in range(NT):
                    last = nc.tensor.transpose(psT[0:E + 1, i * P:(i + 1) * P], cw[:, i, :], ident[:])
                last.then_inc(S["cwtp"], 1)
                prep(pe, "psT_free", b, T_USES, T_USES)
                for i in range(NT):
                    pe.wait_ge(S["psX_free"], SEED + b * X_USES + NT + 1 + i)
                    nc.tensor.matmul(psX[:], cwT[:, i * P:(i + 1) * P], bias_o[:], start=True, stop=True
                                     ).then_inc(S["bmm"], 1)

            def up(k, o, which):
                j, w, b = o % 2, (o // NB) % 2, o % NB
                out = (psA, psB)[which][j]
                if o > 1:
                    pe.wait_ge(S["h_done" if which else "silu_done"], val(k, o, 1, -1))
                for c in range(KC):
                    cols = slice(which * D + c * P, which * D + (c + 1) * P)
                    tok = slice(b * BT, (b + 1) * BT)
                    last = three(out[:], w_hi[w][:, cols], w_lo[w][:, cols], xT_hi[:, c, tok], xT_lo[:, c, tok],
                                 c == 0, c == KC - 1)
                last.then_inc(S["b_ready" if which else "a_ready"], 1)

            def down(k, o, i):
                j, w = (o - 1) % 2, ((o - 1) // NB) % 2
                pe.wait_ge(S["y_free"], val(k, o, NT, -NT + i + 1))
                tok = slice(i * P, (i + 1) * P)
                last = three(psY[i % 2][:], h_hi[j][:, tok], h_lo[j][:, tok], w_hi[w][:, 2 * D:3 * D],
                             w_lo[w][:, 2 * D:3 * D], True, True)
                return last

            def step(k, o):
                if o % NB == 0:
                    pe.wait_ge(S["w_lo_done"], k * 2 + o // NB + 1)
                up(k, o, 0)
                if o > 0:
                    pe.wait_ge(S["lo_done"], val(k, o))
                    down(k, o, 0).then_inc(S["y_ready"], 1)
                    down(k, o, 1).then_inc(S["y_ready"], 1)
                up(k, o, 1)
                if o > 0:
                    down(k, o, 2).then_inc(S["y_ready"], 1)
                    down(k, o, 3).then_inc(S["y_ready"], 1)

            step(0, 0)
            step(0, 1)
            with pe.Fori(0, LOOPS) as k:
                for o in range(2, BODY + 2):
                    step(k, o)
            for o in range(BODY * LOOPS + 2, STEPS):
                step(0, o)
            pe.wait_ge(S["lo_done"], STEPS)
            for i in range(NT):
                down(0, STEPS, i).then_inc(S["y_ready"], 1)


_OUT = (NB, BT, D)


def kernel(x, ctx_2048, g_xattn, g_ffn, L0_ffn_gate_w, L0_ffn_gate_b, L0_ffn_w1, L0_ffn_b1, L0_ffn_w2, L0_ffn_b2,
           L0_ffn_w3, L0_ffn_b3, L0_ffn_ws1, L0_ffn_bs1, L0_ffn_ws2, L0_ffn_bs2, L0_ffn_ws3, L0_ffn_bs3):
    import numpy as np
    import concourse.bacc as bacc
    from concourse.bass_utils import run_bass_kernel_spmd

    def rows(experts, shared):
        a = np.concatenate([np.asarray(experts).reshape(E * H, -1), np.asarray(shared).reshape(HS, -1)])
        return np.concatenate([a, np.zeros((CH * P - HID, a.shape[1]), a.dtype)])

    def up(w):
        return w.reshape(CH, P, KC, P).transpose(0, 3, 2, 1).reshape(CH, P, D)

    w1, w3 = rows(L0_ffn_w1, L0_ffn_ws1), rows(L0_ffn_w3, L0_ffn_ws3)
    w2 = rows(np.asarray(L0_ffn_w2).transpose(0, 2, 1), np.asarray(L0_ffn_ws2).T).reshape(CH, P, D)
    b1 = rows(L0_ffn_b1, L0_ffn_bs1).reshape(CH, P, 1)
    b3 = rows(L0_ffn_b3, L0_ffn_bs3).reshape(CH, P, 1)
    arrays = {
        "x": np.ascontiguousarray(np.asarray(x).reshape(T, D)),
        "ctxT": np.ascontiguousarray(np.asarray(ctx_2048).transpose(0, 2, 1)),
        "g_xattn": np.ascontiguousarray(g_xattn),
        "g_ffn": np.ascontiguousarray(g_ffn),
        "gate_wT": np.ascontiguousarray(np.asarray(L0_ffn_gate_w).T),
        "gate_b": np.ascontiguousarray(L0_ffn_gate_b),
        "w_all": np.ascontiguousarray(np.concatenate([up(w1), up(w3), w2, b1, b3], axis=2)),
        "bias_o": np.ascontiguousarray(np.concatenate([np.asarray(L0_ffn_b2), np.asarray(L0_ffn_bs2)[None]])),
        "ident": np.eye(P, dtype=np.float32),
    }
    nc = bacc.Bacc("TRN2", target_bir_lowering=False, num_devices=1)
    t = {n: nc.dram_tensor(n, a.shape, mybir.dt.from_np(a.dtype), kind="ExternalInput").ap()
         for n, a in arrays.items()}
    t["out"] = nc.dram_tensor("out", (T, D), F32, kind="ExternalOutput").ap()
    build(nc, t)
    r = run_bass_kernel_spmd(nc, [arrays], core_ids=[0])
    return r.results[0]["out"].reshape(_OUT)
```

```python
from contextlib import ExitStack

import concourse.bass as bass
from concourse import mybir

F32 = mybir.dt.float32
F32R = mybir.dt.float32r
I32 = mybir.dt.int32
ALU = mybir.AluOpType
ACT = mybir.ActivationFunctionType
AX = mybir.AxisListType

P = 128
NB = 4
BT = 512
NT = BT // P
T = NB * BT
D = 512
KC = D // P
E = 16
TOP_K = 6
H = 352
HS = 704
HID = E * H + HS
CH = -(-HID // P)
W = 3 * D + 2
UNIT = 32
UPC = P // UNIT
UNITS = CH * UPC
UE = H // UNIT
STEPS = CH * NB
BODY = 2 * NB
LOOPS = (STEPS - 2) // BODY
FP8_MAX = 448.0
ACT_EPS = 1e-4
W_EPS = 1e-6
LN_EPS = 1e-5
EXP_MASK = 0x7F800000
FP8_LEAST = 2.0 ** -6
FP8_ROUND = 1.5 * 2.0 ** 20
ABSENT = -1e30
TAKEN = -3e38
T_USES = 2 * NT + 2
SC = 4
GCH = 7 + 2 * NT
X_USES = 2 * NT + 1


def build(nc, t):
    assert H % UNIT == 0 and HS % UNIT == 0 and CH % 2 == 0
    with ExitStack() as ctx:
        def sb(name, shape, dt=F32):
            return ctx.enter_context(nc.sbuf_tensor(name + "_sb", shape, dt))

        def sem(name):
            return ctx.enter_context(nc.semaphore(name))

        xT_hi = sb("xT_hi", [P, KC, T], F32R)
        xT_lo = sb("xT_lo", [P, KC, T], F32R)
        y = sb("y", [P, T // P, D])
        ident = sb("ident", [P, P])
        bias_o = sb("bias_o", [E + 1, D])
        gate_raw = sb("gate_raw", [P, KC, E])
        gate_hi = sb("gate_hi", [P, KC, P], F32R)
        gate_lo = sb("gate_lo", [P, KC, P], F32R)
        gate_bias = sb("gate_bias", [P, E])
        tanh_g = sb("tanh_g", [P, 2])
        const_half = sb("const_half", [P, 2, NT])

        bias_h = sb("bias_h", [P, 2, 2])
        w_raw = sb("w_raw", [P, W])
        w_hi = [sb(f"w_hi{j}", [P, 3 * D], F32R) for j in range(2)]
        w_lo = [sb(f"w_lo{j}", [P, 3 * D], F32R) for j in range(2)]
        c_bc = sb("c_bc", [P, NB, BT])
        sh = sb("silu_h32", [P, 4, BT])
        silu, h32 = sh[:, 0:2, :], sh[:, 2:4, :]
        h_hi = [sb(f"h_hi{j}", [P, BT], F32R) for j in range(2)]
        h_lo = [sb(f"h_lo{j}", [P, BT], F32R) for j in range(2)]

        ctx_v = sb("ctx_v", [P, KC * D])
        ctx_m = c_bc[:].rearrange("p b n -> p (b n)")
        ctx_hi = sb("ctx_hi", [P, KC, D], F32R)
        ctx_lo = sb("ctx_lo", [P, KC, D], F32R)
        ctx_s = sb("ctx_s", [P, 4, 16])
        xa = sb("xa", [P, NT, D])
        xm = sh
        xs = sb("xs", [P, 4, 16])
        a_hi, a_lo = h_hi, h_lo
        xb = sb("xb", [P, NT, D])
        stat = sb("stat", [P, 2, NT, 6])
        mv = sb("mv", [P, 2, NT, 2])
        rs = sb("rs", [P, 5, 2, NT])
        score = sb("score", [E, BT])
        gt = sb("gt", [P, 3, NT, E])
        biased = sb("biased", [P, 2, NT, E + 2])
        top8 = sb("top8", [P, NT, 8])
        g1 = sb("g1", [P, 3, NT])
        cw = sb("cw", [P, NT, E + 1])
        cwT = sb("cwT", [E + 1, BT])

        cexp = nc.dram_tensor("cexp", [UNITS, T], F32).ap()

        bank = [ctx.enter_context(nc.psum_tensor(f"bank{i}", [P, 512], F32)) for i in range(8)]
        psA, psB, psY = bank[0:2], bank[2:4], bank[4:6]
        psT, psX = bank[6:8], bank[4:6]

        S = {}
        for n in ("gates_in", "x_in", "ctx_in", "set_up", "tanh_done", "gate_hi_done", "gate_lo_done",
                  "cmax", "call", "cscale", "cv", "cm", "cq", "chi", "clo",
                  "st1", "st2", "aggr", "powd", "rstd", "xn1", "xn2", "amax", "xsc", "xv", "xmg", "xq", "xdq",
                  "tp1", "tp2", "t_hi1", "t_hi2", "psT_free", "xmm", "psX_free", "gmm", "gtp", "gch", "gexp", "cwd",
                  "cwtp", "cstored", "bmm",
                  "w_in", "w_hi_done", "w_lo_done", "a_ready", "b_ready", "silu_done",
                  "sc_done", "h_done", "hi_done", "lo_done", "y_ready", "y_free", "stored"):
            S[n] = sem(n)
        SEED, SEEDED = 1, ("tp1", "tp2", "xmm", "gtp", "cwtp", "psT_free", "psX_free")
        c_in = [sem(f"c_in{b}") for b in range(NB)]

        block = ctx.enter_context(nc.Block())

        def val(k, o, per=1, extra=0):
            return k * (BODY * per) + (o * per + extra)

        @block.sync
        def _(sp):
            sp.sem_inc(S["cstored"], 16 * SEED)
            sp.dma_start(y[:, 0:NT, :], t["x"][0:BT].rearrange("(n p) d -> p n d", p=P)).then_inc(S["x_in"], 16)
            sp.dma_start(ctx_v[:].rearrange("p (c n) -> p c n", c=KC),
                         t["ctxT"][0].rearrange("(c p) n -> p c n", p=P)).then_inc(S["ctx_in"], 16)
            sp.dma_start(ident[:], t["ident"]).then_inc(S["gates_in"], 16)
            sp.dma_start(gate_raw[:], t["gate_wT"].rearrange("(c p) e -> p c e", p=P)).then_inc(S["gates_in"], 16)
            sp.dma_start(tanh_g[:, 0:1], t["g_xattn"].partition_broadcast(P)).then_inc(S["gates_in"], 16)
            sp.dma_start(tanh_g[:, 1:2], t["g_ffn"].partition_broadcast(P)).then_inc(S["gates_in"], 16)
            sp.dma_start(gate_bias[:], t["gate_b"].partition_broadcast(P)).then_inc(S["gates_in"], 16)
            sp.dma_start(bias_o[:], t["bias_o"]).then_inc(S["gates_in"], 16)
            sp.dma_start(w_raw[:], t["w_all"][0]).then_inc(S["w_in"], 16)
            x_t = t["x"].rearrange("(b n p) d -> b p n d", p=P, n=NT)
            ctx_t = t["ctxT"].rearrange("b (c p) n -> b p c n", p=P)
            ctx_dst = ctx_v[:].rearrange("p (c n) -> p c n", c=KC)

            def spread_c(b):
                sp.wait_ge(S["psT_free"], SEED + T_USES * (b + 1))
                cols = bass.ds(b * BT, BT)
                sp.dma_start(cexp[0:E * UE, cols].rearrange("(e u) n -> e u n", u=UE),
                             cwT[0:E, :].unsqueeze(1).broadcast_to([E, UE, BT])).then_inc(S["cstored"], 16)
                sp.dma_start(cexp[E * UE:UNITS, cols].rearrange("(e u) n -> e u n", e=1),
                             cwT[E:E + 1, :].unsqueeze(1).broadcast_to([1, UNITS - E * UE, BT])
                             ).then_inc(S["cstored"], 16)

            with sp.Fori(0, NB - 1) as b:
                sp.wait_ge(S["x_in"], 16 * (b + 1))
                sp.dma_start(y[:, bass.ds((b + 1) * NT, NT), :], x_t[bass.ds(b + 1, 1)].squeeze(0)
                             ).then_inc(S["x_in"], 16)
                sp.wait_ge(S["clo"], b + 1)
                sp.dma_start(ctx_dst, ctx_t[bass.ds(b + 1, 1)].squeeze(0)).then_inc(S["ctx_in"], 16)
                spread_c(b)
            spread_c(NB - 1)
            sp.wait_ge(S["cstored"], 16 * SEED + 32 * NB)

            def load_c(g, b):
                src = cexp[bass.ds(g * UPC, UPC), b * BT:(b + 1) * BT]
                sp.dma_start(c_bc[:, b, :], src.unsqueeze(1).broadcast_to([UPC, UNIT, BT])
                             ).then_inc(c_in[b], 16)

            for b in range(NB):
                load_c(0, b)

            def step(k, o):
                b, g = o % NB, k * 2 + o // NB
                sp.wait_ge(S["sc_done"], val(k, o, 1, 1))
                load_c(g + 1, b)
                if b == 2:
                    sp.wait_ge(S["w_lo_done"], g + 2)
                    sp.dma_start(w_raw[:], t["w_all"][bass.ds(g + 2, 1)].squeeze(0)).then_inc(S["w_in"], 16)

            sp.wait_ge(S["w_lo_done"], 1)
            sp.dma_start(w_raw[:], t["w_all"][1]).then_inc(S["w_in"], 16)
            step(0, 0)
            step(0, 1)
            with sp.Fori(0, LOOPS) as k:
                for o in range(2, BODY + 2):
                    step(k, o)
            for o in range(BODY * LOOPS + 2, STEPS - NB):
                sp.wait_ge(S["sc_done"], o + 1)
                load_c(o // NB + 1, o % NB)
            out_t = t["out"].rearrange("(b n p) d -> b p n d", p=P, n=NT)
            for b in range(NB):
                sp.wait_ge(S["y_free"], 2 + NT * (STEPS - NB + b + 1))
                sp.dma_start(out_t[b], y[:, b * NT:(b + 1) * NT, :]).then_inc(S["stored"], 16)
            sp.wait_ge(S["stored"], 16 * NB)

        def wait_apart(e, name, value):
            register = e.to_reg(value)
            e.wait_ge(S["set_up"], 5)
            e.wait_ge(S[name], register)

        def prep(e, name, b, n, per):
            e.wait_ge(S[name], b * per + n + (SEED if name in SEEDED else 0))

        def rounds(e, round_):
            round_(0, True, False)
            with e.Fori(1, NB) as r:
                round_(r, True, True)
            round_(NB, False, True)

        @block.gpsimd
        def _(pool):
            pool.memset(const_half[:], -0.5).then_inc(S["set_up"], 1)
            pool.memset(biased[:], ABSENT).then_inc(S["set_up"], 1)
            pool.memset(gate_hi[:].bitcast(F32), 0.0).then_inc(S["set_up"], 1)
            pool.memset(gate_lo[:].bitcast(F32), 0.0).then_inc(S["set_up"], 1)
            pool.memset(mv[:], 1.0).then_inc(S["set_up"], 1)
            pool.wait_ge(S["set_up"], 5)

            cv16 = ctx_v[:].rearrange("p (q n) -> p q n", n=P)

            def round_(r, first, second):
                wait_apart(pool, "aggr", r + 1)
                pool.tensor_scalar(rs[:, 0], mv[:, :, :, 1], LN_EPS, None, ALU.add).then_inc(S["powd"], 1)
                prep(pool, "powd", r, 1, 2)
                pool.tensor_tensor(rs[:, 1], rs[:, 0], const_half[:], ALU.pow).then_inc(S["powd"], 1)
                if not first:
                    return
                wait_apart(pool, "cmax", r + 1)
                pool.partition_all_reduce(ctx_s[:, 1, :], ctx_s[:, 0, :], P, bass.bass_isa.ReduceOp.max
                                          ).then_inc(S["call"], 1)
                prep(pool, "cscale", r, SC, SC)
                pool.tensor_tensor(cv16, cv16, ctx_s[:, 2, :].unsqueeze(2).broadcast_to([P, 16, P]), ALU.mult
                                   ).then_inc(S["cv"], 1)
                prep(pool, "xmg", r, 2, 2)
                for i in range(NT):
                    pool.tensor_tensor(xa[:, i, :], xa[:, i, :], xm[:, i, :], ALU.add).then_inc(S["xq"], 1)
                for i in range(NT):
                    prep(pool, "xq", r, i + 1, 2 * NT)
                    pool.tensor_tensor(xa[:, i, :], xa[:, i, :], xm[:, i, :], ALU.subtract).then_inc(S["xq"], 1)
                prep(pool, "cm", r, 2, 2)
                pool.tensor_tensor(ctx_v[:], ctx_v[:], ctx_m[:], ALU.add).then_inc(S["cq"], 1)
                prep(pool, "cq", r, 1, 3)
                pool.tensor_tensor(ctx_v[:], ctx_v[:], ctx_m[:], ALU.subtract).then_inc(S["cq"], 1)
                prep(pool, "cq", r, 2, 3)
                pool.tensor_tensor(cv16, cv16, ctx_s[:, 3, :].unsqueeze(2).broadcast_to([P, 16, P]), ALU.mult
                                   ).then_inc(S["cq"], 1)

            rounds(pool, round_)

            def split_lo(g, j):
                pool.wait_ge(S["w_hi_done"], 2 * g + 2)
                pool.tensor_tensor(w_lo[j][:], w_raw[:, 0:3 * D], w_hi[j][:].bitcast(F32), ALU.subtract
                                   ).then_inc(S["w_lo_done"], 1)

            def step(k, o, last=False):
                b, j = o % NB, o % 2
                pool.wait_ge(S["silu_done"], val(k, o, 1, 1))
                pool.wait_ge(c_in[b], (k * 2 + o // NB + 1) * 16)
                pool.tensor_tensor(silu[:, j, :], silu[:, j, :], c_bc[:, b, :], ALU.mult).then_inc(S["sc_done"], 1)
                if b == 2 and not last:
                    split_lo(k * 2 + o // NB + 1, (o // NB + 1) % 2)

            split_lo(0, 0)
            step(0, 0)
            step(0, 1)
            with pool.Fori(0, LOOPS) as k:
                for o in range(2, BODY + 2):
                    step(k, o)
            for o in range(BODY * LOOPS + 2, STEPS):
                step(0, o, last=o >= STEPS - NB)

        @block.scalar
        def _(act):
            def copy(out, in_):
                return nc.scalar.activation(out, in_, ACT.Copy)

            def split_hi(j):
                copy(bias_h[:, j, :], w_raw[:, 3 * D:W]).then_inc(S["w_hi_done"], 1)
                copy(w_hi[j][:], w_raw[:, 0:3 * D]).then_inc(S["w_hi_done"], 1)

            act.wait_ge(S["gates_in"], 16 * 6)
            nc.scalar.activation(tanh_g[:], tanh_g[:], ACT.Tanh).then_inc(S["tanh_done"], 1)
            act.wait_ge(S["set_up"], 5)
            copy(gate_hi[:, :, 0:E], gate_raw[:]).then_inc(S["gate_hi_done"], 1)
            act.wait_ge(S["w_in"], 16)
            split_hi(0)

            def round_(r, first, second):
                b = r - 1
                for i in range(NT if second else 0):
                    prep(act, "tp1", b, i + 1, NT)
                    act.wait_ge(S["xmm"], SEED + b * NT + max(i - 1, 0))
                    copy(a_hi[i % 2][:], psT[i % 2][:]).then_inc(S["t_hi1"], 1)
                prep(act, "rstd", r, 5, 5)
                for half, dst in ((1, xb), (0, xa)):
                    if not (second if half else first):
                        continue
                    act.wait_ge(S["tp2" if half else "tp1"], SEED + b * NT if half else SEED + r * NT)
                    for i in range(NT):
                        row = (b if half else r) * NT + i
                        nc.scalar.activation(dst[:, i, :], y[:, bass.ds(row, 1), :].squeeze(1), ACT.Identity,
                                             bias=rs[:, 4, half, i:i + 1], scale=rs[:, 3, half, i:i + 1]
                                             ).then_inc(S["xn2" if half else "xn1"], 1)
                if second:
                    for i in range(NT):
                        prep(act, "tp2", b, i + 1, NT)
                        copy(xT_hi[:, :, bass.ds(b * BT + i * P, P)],
                             psT[i % 2][:].rearrange("p (c n) -> p c n", c=KC)).then_inc(S["t_hi2"], 1)
                    prep(act, "gmm", b, 1, 1)
                    act.wait_ge(S["gtp"], SEED + b)
                    copy(score[:], psX[0][0:E, :]).then_inc(S["psX_free"], 1)
                    act.wait_ge(S["psT_free"], SEED + b * T_USES + 2 * NT + 1)
                    nc.scalar.activation(gt[:, 1], gt[:, 0], ACT.Exp).then_inc(S["gexp"], 1)
                if first:
                    for i in range(NT):
                        prep(act, "xq", r, NT + i + 1, 2 * NT)
                        for c in range(KC):
                            q = xa[:, i, c * P:(c + 1) * P]
                            nc.scalar.activation(q, q, ACT.Copy, scale=xs[:, 3, i * KC + c:i * KC + c + 1]
                                                 ).then_inc(S["xdq"], 1)
                if second:
                    prep(act, "cwtp", b, 1, 1)
                    act.wait_ge(S["cstored"], 16 * SEED + b * 32)
                    act.wait_ge(S["psX_free"], SEED + b * X_USES)
                    copy(cwT[:], psT[1][0:E + 1, :]).then_inc(S["psT_free"], 1)
                if first:
                    prep(act, "cq", r, 3, 3)
                    act.wait_ge(S["xmm"], SEED + r * NT)
                    copy(ctx_hi[:].rearrange("p c n -> p (c n)"), ctx_v[:]).then_inc(S["chi"], 1)

            rounds(act, round_)

            def step(k, o, last=False):
                b, j = o % NB, o % 2
                g = k * 2 + o // NB
                act.wait_ge(S["a_ready"], val(k, o, 1, 1))
                if o > 1:
                    act.wait_ge(S["h_done"], val(k, o, 1, -1))
                nc.scalar.activation(silu[:, j, :], psA[j][:], ACT.Silu, bias=bias_h[:, (o // NB) % 2, 0:1]
                                     ).then_inc(S["silu_done"], 1)
                if b == 1 and not last:
                    act.wait_ge(S["w_in"], g * 16 + 32)
                    if o > 1:
                        act.wait_ge(S["y_ready"], g * (NB * NT))
                    split_hi((o // NB + 1) % 2)
                act.wait_ge(S["h_done"], val(k, o, 1, 1))
                if o > 1:
                    act.wait_ge(S["y_ready"], val(k, o, NT, -NT))
                copy(h_hi[j][:], h32[:, j, :]).then_inc(S["hi_done"], 1)

            step(0, 0)
            step(0, 1)
            with act.Fori(0, LOOPS) as k:
                for o in range(2, BODY + 2):
                    step(k, o)
            for o in range(BODY * LOOPS + 2, STEPS):
                step(0, o, last=o >= STEPS - NB)

        @block.vector
        def _(dve):
            V = nc.vector
            for n in SEEDED:
                dve.sem_inc(S[n], SEED)
            dve.wait_ge(S["set_up"], 5)
            dve.wait_ge(S["gate_hi_done"], 1)
            V.tensor_tensor(gate_lo[:, :, 0:E], gate_raw[:], gate_hi[:, :, 0:E].bitcast(F32), ALU.subtract
                            ).then_inc(S["gate_lo_done"], 1)
            dve.wait_ge(S["tanh_done"], 1)
            V.tensor_copy(cw[:, :, E:E + 1], tanh_g[:, 1:2].unsqueeze(1).broadcast_to([P, NT, 1])
                          ).then_inc(S["gate_lo_done"], 1)

            def scales(s, name, b):
                prep(dve, name, b, 1, SC)
                V.reciprocal(s[:, 2, :], s[:, 1, :]).then_inc(S[name], 1)
                V.tensor_scalar(s[:, 3, :], s[:, 1, :], 1.0 / FP8_MAX, None, ALU.mult).then_inc(S[name], 1)
                prep(dve, name, b, 2, SC)
                V.tensor_scalar(s[:, 2, :], s[:, 2, :], FP8_MAX, None, ALU.mult).then_inc(S[name], 1)
                prep(dve, name, b, SC, SC)

            def magic(v, m, name, b):
                V.tensor_scalar(m[:].bitcast(I32), v[:].bitcast(I32), EXP_MASK, None, ALU.bitwise_and
                                ).then_inc(S[name], 1)
                prep(dve, name, b, 1, 2)
                V.tensor_scalar(m[:], m[:], FP8_LEAST, FP8_ROUND, ALU.max, ALU.mult).then_inc(S[name], 1)

            xa16 = xa[:].rearrange("p i (c n) -> p (i c) n", n=P)
            cv16 = ctx_v[:].rearrange("p (q n) -> p q n", n=P)

            def round_(r, first, second):
                b = r - 1

                def row(n, i):
                    return y[:, bass.ds(n * NT + i, 1), :].squeeze(1)

                def attention_lo(i):
                    prep(dve, "t_hi1", b, i + 1, NT)
                    dve.wait_ge(S["xmm"], SEED + b * NT + max(i - 1, 0))
                    V.tensor_tensor(a_lo[i % 2][:], psT[i % 2][:],
                                    a_hi[i % 2][:].bitcast(F32), ALU.subtract
                                    ).then_inc(S["psT_free"], 1)

                def residual(i):
                    prep(dve, "xmm", b, i + 1, NT)
                    V.scalar_tensor_tensor(row(b, i), psX[i % 2][:], tanh_g[:, 0:1], row(b, i), ALU.mult, ALU.add
                                           ).then_inc(S["psX_free"], 1)

                def ctx_maxima():
                    dve.wait_ge(S["ctx_in"], (r + 1) * 16)
                    V.tensor_reduce(ctx_s[:, 0, :], cv16, AX.X, ALU.max, apply_absolute_value=True
                                    ).then_inc(S["cmax"], 1)

                def x_statistics():
                    dve.wait_ge(S["x_in"], (r + 1) * 16)
                    for i in range(NT):
                        V.bn_stats(stat[:, 0, i, :], row(r, i)).then_inc(S["st1"], 1)

                if second:
                    attention_lo(0)
                    attention_lo(1)
                if first:
                    ctx_maxima()
                if second:
                    residual(0)
                    attention_lo(2)
                    residual(1)
                    attention_lo(3)
                    residual(2)
                if first:
                    x_statistics()
                if second:
                    residual(3)
                    for i in range(NT):
                        wait_apart(dve, "psX_free", SEED + b * X_USES + i + 1)
                        V.bn_stats(stat[:, 1, i, :], row(b, i)).then_inc(S["st2"], 1)
                for half, n in ((0, r), (1, b)):
                    if not (second if half else first):
                        continue
                    for i in range(NT):
                        wait_apart(dve, "st2" if half else "st1", n * NT + i + 1)
                        last = V.bn_aggr(mv[:, half, i, :], stat[:, half, i, :])
                last.then_inc(S["aggr"], 1)
                if first:
                    prep(dve, "call", r, 1, 1)
                    V.tensor_scalar(ctx_s[:, 1, :], ctx_s[:, 1, :], W_EPS, None, ALU.max).then_inc(S["cscale"], 1)
                    scales(ctx_s, "cscale", r)
                prep(dve, "powd", r, 2, 2)
                V.tensor_tensor(rs[:, 2], rs[:, 1], rs[:, 1], ALU.mult).then_inc(S["rstd"], 1)
                prep(dve, "rstd", r, 1, 5)
                V.tensor_tensor(rs[:, 2], rs[:, 2], rs[:, 0], ALU.mult).then_inc(S["rstd"], 1)
                prep(dve, "rstd", r, 2, 5)
                V.tensor_scalar(rs[:, 2], rs[:, 2], -0.5, 1.5, ALU.mult, ALU.add).then_inc(S["rstd"], 1)
                prep(dve, "rstd", r, 3, 5)
                V.tensor_tensor(rs[:, 3], rs[:, 1], rs[:, 2], ALU.mult).then_inc(S["rstd"], 1)
                prep(dve, "rstd", r, 4, 5)
                V.scalar_tensor_tensor(rs[:, 4], mv[:, :, :, 0], -1.0, rs[:, 3], ALU.mult, ALU.mult
                                       ).then_inc(S["rstd"], 1)

                def expert_lo(i):
                    prep(dve, "t_hi2", b, i + 1, NT)
                    cols = bass.ds(b * BT + i * P, P)
                    V.tensor_tensor(xT_lo[:, :, cols], psT[i % 2][:].rearrange("p (c n) -> p c n", c=KC),
                                    xT_hi[:, :, cols].bitcast(F32), ALU.subtract).then_inc(S["psT_free"], 1)

                if first:
                    prep(dve, "xn1", r, NT, NT)
                    V.tensor_reduce(xs[:, 0, :], xa16, AX.X, ALU.max, apply_absolute_value=True
                                    ).then_inc(S["amax"], 1)
                    prep(dve, "amax", r, 1, 1)
                    V.tensor_scalar(xs[:, 1, :], xs[:, 0, :], ACT_EPS, None, ALU.max).then_inc(S["xsc"], 1)
                    scales(xs, "xsc", r)
                if second:
                    expert_lo(0)
                    expert_lo(1)
                if first:
                    V.tensor_tensor(xa16, xa16, xs[:, 2, :].unsqueeze(2).broadcast_to([P, 16, P]), ALU.mult
                                    ).then_inc(S["xv"], 1)
                if second:
                    expert_lo(2)
                    expert_lo(3)
                if first:
                    prep(dve, "xv", r, 1, 1)
                    magic(xa, xm, "xmg", r)
                    prep(dve, "cv", r, 1, 1)
                    magic(ctx_v, ctx_m, "cm", r)
                if second:
                    routing(b)
                    for i in range(NT):
                        prep(dve, "bmm", b, i + 1, NT)
                        V.tensor_tensor(row(b, i), psX[(i + 1) % 2][:], row(b, i), ALU.add
                                        ).then_inc(S["psX_free"], 1)
                if first:
                    prep(dve, "chi", r, 1, 1)
                    V.tensor_tensor(ctx_lo[:].rearrange("p c n -> p (c n)"), ctx_v[:],
                                    ctx_hi[:].rearrange("p c n -> p (c n)").bitcast(F32), ALU.subtract
                                    ).then_inc(S["clo"], 1)

            def routing(b):
                prep(dve, "gtp", b, 1, 1)
                ps = psT[0][:, 0:NT * E].rearrange("p (i e) -> p i e", e=E)
                V.tensor_reduce(g1[:, 0, :], ps, AX.X, ALU.max).then_inc(S["gch"], 1)
                prep(dve, "gch", b, 1, GCH)
                V.tensor_tensor(gt[:, 0], ps, g1[:, 0, :].unsqueeze(2).broadcast_to([P, NT, E]), ALU.subtract
                                ).then_inc(S["psT_free"], 1)
                prep(dve, "gexp", b, 1, 1)
                V.tensor_reduce(g1[:, 1, :], gt[:, 1], AX.X, ALU.add).then_inc(S["gch"], 1)
                prep(dve, "gch", b, 2, GCH)
                V.reciprocal(g1[:, 2, :], g1[:, 1, :]).then_inc(S["gch"], 1)
                prep(dve, "gch", b, 3, GCH)
                V.tensor_tensor(gt[:, 2], gt[:, 1], g1[:, 2, :].unsqueeze(2).broadcast_to([P, NT, E]), ALU.mult
                                ).then_inc(S["gch"], 1)
                prep(dve, "gch", b, 4, GCH)
                V.tensor_tensor(biased[:, 0, :, 0:E], gt[:, 2], gate_bias[:].unsqueeze(1).broadcast_to([P, NT, E]),
                                ALU.add).then_inc(S["gch"], 1)
                wait_apart(dve, "gch", b * GCH + 5)
                for i in range(NT):
                    V.max(top8[:, i, :], biased[:, 0, i, 0:E]).then_inc(S["gch"], 1)
                prep(dve, "gch", b, 5 + NT, GCH)
                V.memset(top8[:, :, TOP_K:8], ABSENT).then_inc(S["gch"], 1)
                wait_apart(dve, "gch", b * GCH + 6 + NT)
                for i in range(NT):
                    V.match_replace(biased[:, 1, i, :], top8[:, i, :], biased[:, 0, i, :], TAKEN
                                    ).then_inc(S["gch"], 1)
                prep(dve, "gch", b, 6 + 2 * NT, GCH)
                V.scalar_tensor_tensor(gt[:, 0], biased[:, 1, :, 0:E], TAKEN, gt[:, 2], ALU.is_equal, ALU.mult
                                       ).then_inc(S["gch"], 1)
                prep(dve, "gch", b, 7 + 2 * NT, GCH)
                dve.wait_ge(S["cwtp"], SEED + b)
                V.tensor_scalar(cw[:, :, 0:E], gt[:, 0], tanh_g[:, 1:2], None, ALU.mult).then_inc(S["cwd"], 1)

            rounds(dve, round_)
            dve.wait_ge(S["psX_free"], SEED + X_USES * NB)
            dve.nop().then_inc(S["y_free"], 2)

            def add_out(k, o, i):
                dve.wait_ge(S["y_ready"], val(k, o, NT, -NT + i + 1))
                q = ((o - 1) % NB) * NT + i
                V.tensor_tensor(y[:, q, :], psY[i % 2][:], y[:, q, :], ALU.add).then_inc(S["y_free"], 1)

            def step(k, o):
                j = o % 2
                if o > 0:
                    add_out(k, o, 0)
                    add_out(k, o, 1)
                dve.wait_ge(S["b_ready"], val(k, o, 1, 1))
                dve.wait_ge(S["sc_done"], val(k, o, 1, 1))
                if o > 1:
                    dve.wait_ge(S["lo_done"], val(k, o, 1, -1))
                V.scalar_tensor_tensor(h32[:, j, :], psB[j][:], bias_h[:, (o // NB) % 2, 1:2],
                                       silu[:, j, :], ALU.add, ALU.mult).then_inc(S["h_done"], 1)
                if o > 0:
                    add_out(k, o, 2)
                dve.wait_ge(S["hi_done"], val(k, o, 1, 1))
                V.tensor_tensor(h_lo[j][:], h32[:, j, :], h_hi[j][:].bitcast(F32), ALU.subtract
                                ).then_inc(S["lo_done"], 1)
                if o > 0:
                    add_out(k, o, 3)

            step(0, 0)
            step(0, 1)
            with dve.Fori(0, LOOPS) as k:
                for o in range(2, BODY + 2):
                    step(k, o)
            for o in range(BODY * LOOPS + 2, STEPS):
                step(0, o)
            for i in range(NT):
                add_out(0, STEPS, i)

        @block.tensor
        def _(pe):
            def three(out, a_hi, a_lo, b_hi, b_lo, start, stop):
                nc.tensor.matmul(out, a_hi, b_hi, start=start, stop=False)
                nc.tensor.matmul(out, a_hi, b_lo, start=False, stop=False)
                return nc.tensor.matmul(out, a_lo, b_hi, start=False, stop=stop)

            pe.wait_ge(S["gates_in"], 16 * 6)
            pe.wait_ge(S["gate_lo_done"], 2)

            def round_(r, first, second):
                if not second:
                    return
                b = r - 1

                def t_free(n):
                    pe.wait_ge(S["psT_free"], SEED + b * T_USES + max(n - 1, 0))

                def x_free(n):
                    pe.wait_ge(S["psX_free"], SEED + b * X_USES + max(n - 1, 0))

                def transposes(i, src, name, per, signal, use):
                    prep(pe, name, b, per * (i + 1), per * NT)
                    t_free(use)
                    for c in range(KC):
                        last = nc.tensor.transpose(psT[i % 2][:, c * P:(c + 1) * P],
                                                   src[:, i, c * P:(c + 1) * P], ident[:])
                    last.then_inc(S[signal], 1)

                def attend(i):
                    prep(pe, "psT_free", b, i + 1, T_USES)
                    prep(pe, "clo", b, 1, 1)
                    x_free(i)
                    for c in range(KC):
                        last = three(psX[i % 2][:], a_hi[i % 2][:, c * P:(c + 1) * P], a_lo[i % 2][:, c * P:(c + 1) * P], ctx_hi[:, c, :],
                                     ctx_lo[:, c, :], c == 0, c == KC - 1)
                    last.then_inc(S["xmm"], 1)

                for i in range(NT):
                    transposes(i, xa, "xdq", KC, "tp1", i)
                    if i:
                        attend(i - 1)
                attend(NT - 1)
                for i in range(NT):
                    transposes(i, xb, "xn2", 1, "tp2", NT + i)
                pe.wait_ge(S["psT_free"], SEED + b * T_USES + 2 * NT)
                x_free(NT)
                cols = bass.ds(b * BT, BT)
                for c in range(KC):
                    last = three(psX[0][:], gate_hi[:, c, :], gate_lo[:, c, :], xT_hi[:, c, cols],
                                 xT_lo[:, c, cols], c == 0, c == KC - 1)
                last.then_inc(S["gmm"], 1)
                wait_apart(pe, "psX_free", SEED + b * X_USES + NT + 1)
                for i in range(NT):
                    last = nc.tensor.transpose(psT[0][:, i * E:(i + 1) * E], score[:, i * P:(i + 1) * P],
                                               ident[0:E, 0:E])
                last.then_inc(S["gtp"], 1)
                prep(pe, "cwd", b, 1, 1)
                for i in range(NT):
                    last = nc.tensor.transpose(psT[1][0:E + 1, i * P:(i + 1) * P], cw[:, i, :], ident[:])
                last.then_inc(S["cwtp"], 1)
                prep(pe, "psT_free", b, T_USES, T_USES)
                for i in range(NT):
                    x_free(NT + 1 + i)
                    nc.tensor.matmul(psX[(i + 1) % 2][:], cwT[:, i * P:(i + 1) * P], bias_o[:], start=True,
                                     stop=True).then_inc(S["bmm"], 1)

            rounds(pe, round_)

            def up(k, o, which):
                j, w, b = o % 2, (o // NB) % 2, o % NB
                out = (psA, psB)[which][j]
                if o > 1:
                    pe.wait_ge(S["h_done" if which else "silu_done"], val(k, o, 1, -1))
                for c in range(KC):
                    cols = slice(which * D + c * P, which * D + (c + 1) * P)
                    tok = slice(b * BT, (b + 1) * BT)
                    last = three(out[:], w_hi[w][:, cols], w_lo[w][:, cols], xT_hi[:, c, tok], xT_lo[:, c, tok],
                                 c == 0, c == KC - 1)
                last.then_inc(S["b_ready" if which else "a_ready"], 1)

            def down(k, o, i):
                j, w = (o - 1) % 2, ((o - 1) // NB) % 2
                pe.wait_ge(S["y_free"], val(k, o, NT, -NT + i + 1))
                tok = slice(i * P, (i + 1) * P)
                last = three(psY[i % 2][:], h_hi[j][:, tok], h_lo[j][:, tok], w_hi[w][:, 2 * D:3 * D],
                             w_lo[w][:, 2 * D:3 * D], True, True)
                return last

            def step(k, o):
                if o % NB == 0:
                    pe.wait_ge(S["w_lo_done"], k * 2 + o // NB + 1)
                up(k, o, 0)
                if o > 0:
                    pe.wait_ge(S["lo_done"], val(k, o))
                    down(k, o, 0).then_inc(S["y_ready"], 1)
                    down(k, o, 1).then_inc(S["y_ready"], 1)
                up(k, o, 1)
                if o > 0:
                    down(k, o, 2).then_inc(S["y_ready"], 1)
                    down(k, o, 3).then_inc(S["y_ready"], 1)

            step(0, 0)
            step(0, 1)
            with pe.Fori(0, LOOPS) as k:
                for o in range(2, BODY + 2):
                    step(k, o)
            for o in range(BODY * LOOPS + 2, STEPS):
                step(0, o)
            pe.wait_ge(S["lo_done"], STEPS)
            for i in range(NT):
                down(0, STEPS, i).then_inc(S["y_ready"], 1)


_OUT = (NB, BT, D)


def kernel(x, ctx_2048, g_xattn, g_ffn, L0_ffn_gate_w, L0_ffn_gate_b, L0_ffn_w1, L0_ffn_b1, L0_ffn_w2, L0_ffn_b2,
           L0_ffn_w3, L0_ffn_b3, L0_ffn_ws1, L0_ffn_bs1, L0_ffn_ws2, L0_ffn_bs2, L0_ffn_ws3, L0_ffn_bs3):
    import numpy as np
    import concourse.bacc as bacc
    from concourse.bass_utils import run_bass_kernel_spmd

    def rows(experts, shared):
        a = np.concatenate([np.asarray(experts).reshape(E * H, -1), np.asarray(shared).reshape(HS, -1)])
        return np.concatenate([a, np.zeros((CH * P - HID, a.shape[1]), a.dtype)])

    def up(w):
        return w.reshape(CH, P, KC, P).transpose(0, 3, 2, 1).reshape(CH, P, D)

    w1, w3 = rows(L0_ffn_w1, L0_ffn_ws1), rows(L0_ffn_w3, L0_ffn_ws3)
    w2 = rows(np.asarray(L0_ffn_w2).transpose(0, 2, 1), np.asarray(L0_ffn_ws2).T).reshape(CH, P, D)
    b1 = rows(L0_ffn_b1, L0_ffn_bs1).reshape(CH, P, 1)
    b3 = rows(L0_ffn_b3, L0_ffn_bs3).reshape(CH, P, 1)
    arrays = {
        "x": np.ascontiguousarray(np.asarray(x).reshape(T, D)),
        "ctxT": np.ascontiguousarray(np.asarray(ctx_2048).transpose(0, 2, 1)),
        "g_xattn": np.ascontiguousarray(g_xattn),
        "g_ffn": np.ascontiguousarray(g_ffn),
        "gate_wT": np.ascontiguousarray(np.asarray(L0_ffn_gate_w).T),
        "gate_b": np.ascontiguousarray(L0_ffn_gate_b),
        "w_all": np.ascontiguousarray(np.concatenate([up(w1), up(w3), w2, b1, b3], axis=2)),
        "bias_o": np.ascontiguousarray(np.concatenate([np.asarray(L0_ffn_b2), np.asarray(L0_ffn_bs2)[None]])),
        "ident": np.eye(P, dtype=np.float32),
    }
    nc = bacc.Bacc("TRN2", target_bir_lowering=False, num_devices=1)
    t = {n: nc.dram_tensor(n, a.shape, mybir.dt.from_np(a.dtype), kind="ExternalInput").ap()
         for n, a in arrays.items()}
    t["out"] = nc.dram_tensor("out", (T, D), F32, kind="ExternalOutput").ap()
    build(nc, t)
    r = run_bass_kernel_spmd(nc, [arrays], core_ids=[0])
    return r.results[0]["out"].reshape(_OUT)
```

```python
from contextlib import ExitStack

import concourse.bass as bass
from concourse import mybir

F32 = mybir.dt.float32
F32R = mybir.dt.float32r
I32 = mybir.dt.int32
ALU = mybir.AluOpType
ACT = mybir.ActivationFunctionType
AX = mybir.AxisListType

P = 128
NB = 4
BT = 512
NT = BT // P
T = NB * BT
D = 512
KC = D // P
E = 16
TOP_K = 6
H = 352
HS = 704
HID = E * H + HS
CH = -(-HID // P)
W = 3 * D + 2
UNIT = 32
UPC = P // UNIT
UNITS = CH * UPC
UE = H // UNIT
SPARE_B1 = 2.0 ** 7
BIAS_ROW = HID - (CH - 1) * P
STEPS = CH * NB
BODY = 2 * NB
EARLY = 3
LOOPS = (STEPS - EARLY) // BODY
FP8_MAX = 448.0
ACT_EPS = 1e-4
W_EPS = 1e-6
LN_EPS = 1e-5
EXP_MASK = 0x7F800000
FP8_LEAST = 2.0 ** -6
FP8_ROUND = 1.5 * 2.0 ** 20
ABSENT = -1e30
TAKEN = -3e38
T_USES = 2 * NT
SC = 4
GCH = 7 + 2 * NT
X_USES = NT + 1


def build(nc, t):
    assert H % UNIT == 0 and HS % UNIT == 0 and CH % 2 == 0
    with ExitStack() as ctx:
        def sb(name, shape, dt=F32):
            return ctx.enter_context(nc.sbuf_tensor(name + "_sb", shape, dt))

        def sem(name):
            return ctx.enter_context(nc.semaphore(name))

        xT_hi = sb("xT_hi", [P, KC, T], F32R)
        xT_lo = sb("xT_lo", [P, KC, T], F32R)
        y = sb("y", [P, T // P, D])
        ident = sb("ident", [P, P])
        gate_raw = sb("gate_raw", [P, KC, E])
        gate_hi = sb("gate_hi", [P, KC, P], F32R)
        gate_lo = sb("gate_lo", [P, KC, P], F32R)
        gate_bias = sb("gate_bias", [P, E])
        tanh_g = sb("tanh_g", [P, 2])
        const_half = sb("const_half", [P, 2, NT])

        bias_h = sb("bias_h", [P, 2, 2])
        w_raw = sb("w_raw", [P, W])
        w_hi = [sb(f"w_hi{j}", [P, 3 * D], F32R) for j in range(2)]
        w_lo = [sb(f"w_lo{j}", [P, 3 * D], F32R) for j in range(2)]
        c_bc = sb("c_bc", [P, NB, BT])
        sh = sb("silu_h32", [P, 4, BT])
        silu, h32 = sh[:, 0:2, :], sh[:, 2:4, :]
        h_hi = [sb(f"h_hi{j}", [P, BT], F32R) for j in range(2)]
        h_lo = [sb(f"h_lo{j}", [P, BT], F32R) for j in range(2)]

        ctx_v = sb("ctx_v", [P, KC * D])
        ctx_m = c_bc[:].rearrange("p b n -> p (b n)")
        ctx_hi = sb("ctx_hi", [P, KC, D], F32R)
        ctx_lo = sb("ctx_lo", [P, KC, D], F32R)
        ctx_s = sb("ctx_s", [P, 4, 16])
        xa = sb("xa", [P, NT, D])
        xm = sh
        xs = sb("xs", [P, 4, 16])
        a_hi, a_lo = h_hi, h_lo
        xb = sb("xb", [P, NT, D])
        stat = sb("stat", [P, 2, NT, 6])
        mv = sb("mv", [P, 2, NT, 2])
        rs = sb("rs", [P, 5, 2, NT])
        score = sb("score", [E, BT])
        gt = sb("gt", [P, 3, NT, E])
        biased = sb("biased", [P, 2, NT, E + 2])
        top8 = sb("top8", [P, NT, 8])
        g1 = sb("g1", [P, 3, NT])
        cw = sb("cw", [P, NT, E + 1])
        cwT = sb("cwT", [E + 1, BT])

        cexp = nc.dram_tensor("cexp", [UNITS, T], F32).ap()

        bank = [ctx.enter_context(nc.psum_tensor(f"bank{i}", [P, 512], F32)) for i in range(8)]
        psA, psB, psY = bank[0:2], bank[2:4], bank[4:6]
        psT = bank[6], bank[7], bank[1], bank[3]
        psX = bank[4:6]

        def expert_banks(first):
            return (psT, psX) if first else (psT[0:2] + tuple(psX), psT[0:2])

        S = {}
        for n in ("gates_in", "x_in", "ctx_in", "set_up", "tanh_done", "gate_hi_done", "gate_lo_done",
                  "cmax", "call", "cscale", "cv", "cm", "cq", "cdq", "chi", "clo",
                  "st1", "st2", "aggr", "powd", "rstd", "xn1", "xn2", "amax", "xsc", "xv", "xmg", "xq", "xdq",
                  "tp1", "tp2", "t_hi1", "t_hi2", "psT_free", "xmm", "psX_free", "gmm", "gtp", "gch", "gexp", "cwd",
                  "gsub", "cwtp", "cwt_free", "cstored",
                  "w_in", "w_hi_done", "w_lo_done", "a_ready", "b_ready", "silu_done",
                  "sc_done", "h_done", "hi_done", "lo_done", "y_ready", "y_free", "stored"):
            S[n] = sem(n)
        SEED, SEEDED = 1, ("tp1", "tp2", "xmm", "gtp", "cwt_free", "psT_free", "psX_free")
        c_in = [sem(f"c_in{b}") for b in range(NB)]

        block = ctx.enter_context(nc.Block())

        def val(k, o, per=1, extra=0):
            return k * (BODY * per) + (o * per + extra)

        @block.sync
        def _(sp):
            sp.sem_inc(S["cstored"], 16 * SEED)
            sp.dma_start(ctx_v[:].rearrange("p (c n) -> p c n", c=KC),
                         t["ctxT"][0].rearrange("(c p) n -> p c n", p=P)).then_inc(S["ctx_in"], 16)
            sp.dma_start(y[:, 0:NT, :], t["x"][0:BT].rearrange("(n p) d -> p n d", p=P)).then_inc(S["x_in"], 16)
            sp.dma_start(ident[:], t["ident"]).then_inc(S["gates_in"], 16)
            sp.dma_start(gate_raw[:], t["gate_wT"].rearrange("(c p) e -> p c e", p=P)).then_inc(S["gates_in"], 16)
            sp.dma_start(tanh_g[:, 0:1], t["g_xattn"].partition_broadcast(P)).then_inc(S["gates_in"], 16)
            sp.dma_start(tanh_g[:, 1:2], t["g_ffn"].partition_broadcast(P)).then_inc(S["gates_in"], 16)
            sp.dma_start(gate_bias[:], t["gate_b"].partition_broadcast(P)).then_inc(S["gates_in"], 16)
            sp.dma_start(w_raw[:], t["w_all"][0]).then_inc(S["w_in"], 16)
            x_t = t["x"].rearrange("(b n p) d -> b p n d", p=P, n=NT)
            ctx_t = t["ctxT"].rearrange("b (c p) n -> b p c n", p=P)
            ctx_dst = ctx_v[:].rearrange("p (c n) -> p c n", c=KC)

            def spread_c(b):
                sp.wait_ge(S["cwt_free"], SEED + b + 1)
                cols = bass.ds(b * BT, BT)
                sp.dma_start(cexp[0:E * UE, cols].rearrange("(e u) n -> e u n", u=UE),
                             cwT[0:E, :].unsqueeze(1).broadcast_to([E, UE, BT])).then_inc(S["cstored"], 16)
                sp.dma_start(cexp[E * UE:UNITS, cols].rearrange("(e u) n -> e u n", e=1),
                             cwT[E:E + 1, :].unsqueeze(1).broadcast_to([1, UNITS - E * UE, BT])
                             ).then_inc(S["cstored"], 16)

            for b in range(1, NB):
                sp.wait_ge(S["x_in"], 16 * b)
                sp.dma_start(y[:, b * NT:(b + 1) * NT, :], x_t[b]).then_inc(S["x_in"], 16)

            def load_ctx(b):
                sp.wait_ge(S["clo"], b)
                sp.dma_start(ctx_dst, ctx_t[bass.ds(b, 1)].squeeze(0)).then_inc(S["ctx_in"], 16)

            load_ctx(1)
            with sp.Fori(2, NB) as b:
                load_ctx(b)
                spread_c(b - 2)
            spread_c(NB - 2)

            def load_c(g, b):
                src = cexp[bass.ds(g * UPC, UPC), b * BT:(b + 1) * BT]
                sp.dma_start(c_bc[:, b, :], src.unsqueeze(1).broadcast_to([UPC, UNIT, BT])
                             ).then_inc(c_in[b], 16)

            sp.wait_ge(S["w_lo_done"], 1)
            sp.dma_start(w_raw[:], t["w_all"][1]).then_inc(S["w_in"], 16)
            sp.wait_ge(S["cstored"], 16 * SEED + 32 * (NB - 1))
            sp.wait_ge(S["cq"], 4 * NB)
            for b in range(NB - 1):
                load_c(0, b)
            spread_c(NB - 1)
            sp.wait_ge(S["cstored"], 16 * SEED + 32 * NB)
            load_c(0, NB - 1)

            def step(k, o):
                b, g = o % NB, k * 2 + o // NB
                sp.wait_ge(S["sc_done"], val(k, o, 1, 1))
                load_c(g + 1, b)
                if b == 2:
                    sp.wait_ge(S["w_lo_done"], g + 2)
                    sp.dma_start(w_raw[:], t["w_all"][bass.ds(g + 2, 1)].squeeze(0)).then_inc(S["w_in"], 16)

            step(0, 0)
            step(0, 1)
            with sp.Fori(0, LOOPS) as k:
                for o in range(2, BODY + 2):
                    step(k, o)
            for o in range(BODY * LOOPS + 2, STEPS - NB):
                sp.wait_ge(S["sc_done"], o + 1)
                load_c(o // NB + 1, o % NB)
            for b in range(NB):
                sp.wait_ge(c_in[b], 16 * CH)
                own = cexp[0:E * UE, b * BT:(b + 1) * BT].rearrange("(e u) n -> e u n", u=UE)[:, 0, :]
                sp.dma_start(c_bc[BIAS_ROW:BIAS_ROW + E, b, :], own).then_inc(c_in[b], 16)
            out_t = t["out"].rearrange("(b n p) d -> b p n d", p=P, n=NT)
            for b in range(NB - 1):
                sp.wait_ge(S["y_free"], 2 + NT * (STEPS - NB + b + 1))
                sp.dma_start(out_t[b], y[:, b * NT:(b + 1) * NT, :]).then_inc(S["stored"], 16)
            for i in range(NT):
                sp.wait_ge(S["y_free"], 2 + NT * (STEPS - 1) + i + 1)
                sp.dma_start(out_t[NB - 1][:, i, :], y[:, (NB - 1) * NT + i, :]).then_inc(S["stored"], 16)
            sp.wait_ge(S["stored"], 16 * (NB - 1 + NT))

        def wait_apart(e, name, value):
            register = e.to_reg(value)
            e.wait_ge(S["set_up"], 5)
            e.wait_ge(S[name], register)

        def half(v, h):
            n = KC * D // 2
            return v[:, h * n:(h + 1) * n]

        def prep(e, name, b, n, per):
            e.wait_ge(S[name], b * per + n + (SEED if name in SEEDED else 0))

        def rounds(e, round_):
            round_(0, True, False, True)
            with e.Fori(1, NB - 1) as r:
                round_(r, True, True, True)
            round_(NB - 1, True, True, False)
            round_(NB, False, True, False)

        @block.gpsimd
        def _(pool):
            pool.memset(const_half[:], -0.5).then_inc(S["set_up"], 1)
            pool.memset(biased[:], ABSENT).then_inc(S["set_up"], 1)
            pool.memset(gate_hi[:].bitcast(F32), 0.0).then_inc(S["set_up"], 1)
            pool.memset(gate_lo[:].bitcast(F32), 0.0).then_inc(S["set_up"], 1)
            pool.memset(mv[:], 1.0).then_inc(S["set_up"], 1)
            pool.wait_ge(S["set_up"], 5)

            def power(r):
                wait_apart(pool, "aggr", r + 1)
                pool.tensor_scalar(rs[:, 0], mv[:, :, :, 1], LN_EPS, None, ALU.add).then_inc(S["powd"], 1)
                prep(pool, "powd", r, 1, 2)
                pool.tensor_tensor(rs[:, 1], rs[:, 0], const_half[:], ALU.pow).then_inc(S["powd"], 1)

            def split_lo(g, j):
                pool.wait_ge(S["w_hi_done"], 2 * g + 2)
                pool.tensor_tensor(w_lo[j][:], w_raw[:, 0:3 * D], w_hi[j][:].bitcast(F32), ALU.subtract
                                   ).then_inc(S["w_lo_done"], 1)

            def grid_x(r, i):
                prep(pool, "xmg", r, 3 + i // 2, 4)
                for k, op in ((0, ALU.add), (2, ALU.subtract)):
                    for j in (i, i + 1):
                        if k:
                            prep(pool, "xq", r, 2 * i + j - i + 1, 2 * NT)
                        pool.tensor_tensor(xa[:, j, :], xa[:, j, :], xm[:, j, :], op).then_inc(S["xq"], 1)

            def grid_ctx(r, h):
                v, m = half(ctx_v, h), half(ctx_m, h)
                prep(pool, "cm", r, 3 + h, 4)
                pool.tensor_tensor(v, v, m, ALU.add).then_inc(S["cq"], 1)
                prep(pool, "cq", r, 2 * h + 1, 4)
                pool.tensor_tensor(v, v, m, ALU.subtract).then_inc(S["cq"], 1)

            def step(k, o, last=False):
                b, j = o % NB, o % 2
                pool.wait_ge(S["silu_done"], val(k, o, 1, 1))
                pool.wait_ge(c_in[b], (k * 2 + o // NB + 1 + (1 if last else 0)) * 16)
                pool.tensor_tensor(silu[:, j, :], silu[:, j, :], c_bc[:, b, :], ALU.mult).then_inc(S["sc_done"], 1)
                if b == 2 and not last:
                    split_lo(k * 2 + o // NB + 1, (o // NB + 1) % 2)

            def round_(r, first, second, after):
                if first:
                    wait_apart(pool, "cmax", r + 1)
                    pool.partition_all_reduce(ctx_s[:, 1, :], ctx_s[:, 0, :], P, bass.bass_isa.ReduceOp.max
                                              ).then_inc(S["call"], 1)
                if not second:
                    power(r)
                if not first:
                    split_lo(0, 0)
                if first:
                    grid_ctx(r, 0)
                if second:
                    power(r + 1)
                if first:
                    grid_ctx(r, 1)
                    grid_x(r, 0)
                if not second:
                    power(r + 1)
                if first:
                    grid_x(r, 2)
                else:
                    for o in range(EARLY):
                        step(0, o)

            rounds(pool, round_)

            with pool.Fori(0, LOOPS) as k:
                for o in range(EARLY, BODY + EARLY):
                    step(k, o)
            for o in range(BODY * LOOPS + EARLY, STEPS):
                step(0, o, last=o >= STEPS - NB)

        @block.scalar
        def _(act):
            def copy(out, in_):
                return nc.scalar.activation(out, in_, ACT.Copy)

            def split_hi(j):
                copy(bias_h[:, j, :], w_raw[:, 3 * D:W]).then_inc(S["w_hi_done"], 1)
                copy(w_hi[j][:], w_raw[:, 0:3 * D]).then_inc(S["w_hi_done"], 1)

            def blockwise(x, scale, q):
                for c in q:
                    v = x[:, c * P:(c + 1) * P]
                    last = nc.scalar.activation(v, v, ACT.Copy, scale=scale[:, c:c + 1])
                return last

            xa_flat = xa[:].rearrange("p i d -> p (i d)")

            def normalise(dst, n, half, i):
                nc.scalar.activation(dst[:, i, :], y[:, bass.ds(n * NT + i, 1), :].squeeze(1), ACT.Identity,
                                     bias=rs[:, 4, half, i:i + 1], scale=rs[:, 3, half, i:i + 1]
                                     ).then_inc(S["xn2" if half else "xn1"], 1)

            def silu_(k, o):
                act.wait_ge(S["a_ready"], val(k, o, 1, 1))
                if o > 1:
                    act.wait_ge(S["h_done"], val(k, o, 1, -1))
                nc.scalar.activation(silu[:, o % 2, :], psA[o % 2][:], ACT.Silu, bias=bias_h[:, (o // NB) % 2, 0:1]
                                     ).then_inc(S["silu_done"], 1)

            def split_next(k, o):
                g = k * 2 + o // NB
                act.wait_ge(S["w_in"], g * 16 + 32)
                if o > 1:
                    act.wait_ge(S["y_ready"], g * (NB * NT))
                split_hi((o // NB + 1) % 2)

            def hidden_hi(k, o):
                act.wait_ge(S["h_done"], val(k, o, 1, 1))
                if o > 1:
                    act.wait_ge(S["y_ready"], val(k, o, NT, -NT))
                copy(h_hi[o % 2][:], h32[:, o % 2, :]).then_inc(S["hi_done"], 1)

            def round_(r, first, second, after):
                b = r - 1
                psE, psG = expert_banks(first)

                def attention_hi(b, i):
                    prep(act, "tp1", b, i + 1, NT)
                    act.wait_ge(S["xmm"], SEED + b * NT + max(i - 1, 0))
                    copy(a_hi[i % 2][:], psT[i][:]).then_inc(S["t_hi1"], 1)

                def scale_ctx(h):
                    if h == 0:
                        prep(act, "cscale", r, SC, SC)
                    blockwise(ctx_v, ctx_s[:, 2, :], range(8 * h, 8 * h + 8)).then_inc(S["cv"], 1)

                def unscale_ctx(h):
                    prep(act, "cq", r, 2 * h + 2, 4)
                    blockwise(ctx_v, ctx_s[:, 3, :], range(8 * h, 8 * h + 8)).then_inc(S["cdq"], 1)

                def unscale_x(i):
                    prep(act, "xq", r, 4 * (i // 2) + 3 + i % 2, 2 * NT)
                    blockwise(xa_flat, xs[:, 3, :], range(i * KC, (i + 1) * KC)).then_inc(S["xdq"], 1)

                if second:
                    attention_hi(b, 2)
                if first:
                    if not second:
                        scale_ctx(0)
                        scale_ctx(1)
                    prep(act, "rstd", r, 5, 5)
                    act.wait_ge(S["tp1"], SEED + r * NT)
                    for i in range(2):
                        normalise(xa, r, 0, i)
                    if second:
                        scale_ctx(0)
                        attention_hi(b, 3)
                        scale_ctx(1)
                    for i in range(2, NT):
                        normalise(xa, r, 0, i)
                else:
                    attention_hi(b, 3)
                    silu_(0, 0)
                if not second:
                    act.wait_ge(S["gates_in"], 16 * 5)
                    nc.scalar.activation(tanh_g[:], tanh_g[:], ACT.Tanh).then_inc(S["tanh_done"], 1)
                    act.wait_ge(S["set_up"], 5)
                    copy(gate_hi[:, :, 0:E], gate_raw[:]).then_inc(S["gate_hi_done"], 1)
                    act.wait_ge(S["w_in"], 16)
                    split_hi(0)
                if first:
                    unscale_ctx(0)
                if second:
                    prep(act, "rstd", r + 1, 5, 5)
                    act.wait_ge(S["tp2"], SEED + b * NT)
                    for i in range(NT):
                        normalise(xb, b, 1, i)
                    for i in range(NT):
                        prep(act, "tp2", b, i + 1, NT)
                        copy(xT_hi[:, :, bass.ds(b * BT + i * P, P)],
                             psE[i][:].rearrange("p (c n) -> p c n", c=KC)).then_inc(S["t_hi2"], 1)
                if not first:
                    act.wait_ge(S["xmm"], SEED + NB * NT)
                    hidden_hi(0, 0)
                    silu_(0, 1)
                    hidden_hi(0, 1)
                if first:
                    unscale_ctx(1)
                    prep(act, "cdq", r, 2, 2)
                    act.wait_ge(S["xmm"], SEED + r * NT)
                    copy(ctx_hi[:].rearrange("p c n -> p (c n)"), ctx_v[:]).then_inc(S["chi"], 1)
                    unscale_x(0)
                    unscale_x(1)
                if second:
                    prep(act, "gmm", b, 1, 1)
                    act.wait_ge(S["gtp"], SEED + b)
                    copy(score[:], psG[0][0:E, :]).then_inc(S["psX_free"], 1)
                if first:
                    attention_hi(r, 0)
                    attention_hi(r, 1)
                if second:
                    prep(act, "gsub", b, 1, 1)
                    nc.scalar.activation(gt[:, 1], gt[:, 0], ACT.Exp).then_inc(S["gexp"], 1)
                if first:
                    unscale_x(2)
                    unscale_x(3)
                else:
                    split_next(0, 1)
                    silu_(0, 2)
                if second:
                    prep(act, "cwtp", b, 1, 1)
                    act.wait_ge(S["cstored"], 16 * SEED + b * 32)
                    copy(cwT[:], psT[0][0:E + 1, :]).then_inc(S["cwt_free"], 1)

            rounds(act, round_)

            def step(k, o, last=False):
                silu_(k, o)
                if o % NB == 1 and not last:
                    split_next(k, o)
                hidden_hi(k, o)

            hidden_hi(0, EARLY - 1)
            with act.Fori(0, LOOPS) as k:
                for o in range(EARLY, BODY + EARLY):
                    step(k, o)
            for o in range(BODY * LOOPS + EARLY, STEPS):
                step(0, o, last=o >= STEPS - NB)

        @block.vector
        def _(dve):
            V = nc.vector
            for n in SEEDED:
                dve.sem_inc(S[n], SEED)
            dve.wait_ge(S["set_up"], 5)

            def scales(s, name, b):
                prep(dve, name, b, 1, SC)
                V.reciprocal(s[:, 2, :], s[:, 1, :]).then_inc(S[name], 1)
                V.tensor_scalar(s[:, 3, :], s[:, 1, :], 1.0 / FP8_MAX, None, ALU.mult).then_inc(S[name], 1)
                prep(dve, name, b, 2, SC)
                V.tensor_scalar(s[:, 2, :], s[:, 2, :], FP8_MAX, None, ALU.mult).then_inc(S[name], 1)
                prep(dve, name, b, SC, SC)

            def magic(v, m, name, b):
                for h in range(2):
                    V.tensor_scalar(half(m, h).bitcast(I32), half(v, h).bitcast(I32), EXP_MASK, None,
                                    ALU.bitwise_and).then_inc(S[name], 1)
                for h in range(2):
                    prep(dve, name, b, 1 + h, 4)
                    V.tensor_scalar(half(m, h), half(m, h), FP8_LEAST, FP8_ROUND, ALU.max, ALU.mult
                                    ).then_inc(S[name], 1)

            xa_flat = xa[:].rearrange("p i d -> p (i d)")
            xm_flat = xm[:].rearrange("p i d -> p (i d)")
            xa16 = xa[:].rearrange("p i (c n) -> p (i c) n", n=P)
            cv16 = ctx_v[:].rearrange("p (q n) -> p q n", n=P)

            def row(n, i):
                return y[:, bass.ds(n * NT + i, 1), :].squeeze(1)

            def x_statistics(n):
                dve.wait_ge(S["x_in"], (n + 1) * 16)
                for i in range(NT):
                    V.bn_stats(stat[:, 0, i, :], row(n, i)).then_inc(S["st1"], 1)

            def aggregate(r, first, second):
                for half, n in ((0, r), (1, r - 2)):
                    for i in range(NT if (second if half else first) else 0):
                        wait_apart(dve, "st2" if half else "st1", n * NT + i + 1)
                        last = V.bn_aggr(mv[:, half, i, :], stat[:, half, i, :])
                last.then_inc(S["aggr"], 1)

            def deviation(r):
                prep(dve, "powd", r, 2, 2)
                V.tensor_tensor(rs[:, 2], rs[:, 1], rs[:, 1], ALU.mult).then_inc(S["rstd"], 1)
                prep(dve, "rstd", r, 1, 5)
                V.tensor_tensor(rs[:, 2], rs[:, 2], rs[:, 0], ALU.mult).then_inc(S["rstd"], 1)
                prep(dve, "rstd", r, 2, 5)
                V.tensor_scalar(rs[:, 2], rs[:, 2], -0.5, 1.5, ALU.mult, ALU.add).then_inc(S["rstd"], 1)
                prep(dve, "rstd", r, 3, 5)
                V.tensor_tensor(rs[:, 3], rs[:, 1], rs[:, 2], ALU.mult).then_inc(S["rstd"], 1)
                prep(dve, "rstd", r, 4, 5)
                V.scalar_tensor_tensor(rs[:, 4], mv[:, :, :, 0], -1.0, rs[:, 3], ALU.mult, ALU.mult
                                       ).then_inc(S["rstd"], 1)

            def add_out(k, o, i):
                dve.wait_ge(S["y_ready"], val(k, o, NT, -NT + i + 1))
                q = ((o - 1) % NB) * NT + i
                V.tensor_tensor(y[:, q, :], psY[i % 2][:], y[:, q, :], ALU.add).then_inc(S["y_free"], 1)

            def hidden(k, o):
                j = o % 2
                dve.wait_ge(S["b_ready"], val(k, o, 1, 1))
                dve.wait_ge(S["sc_done"], val(k, o, 1, 1))
                if o > 1:
                    dve.wait_ge(S["lo_done"], val(k, o, 1, -1))
                V.scalar_tensor_tensor(h32[:, j, :], psB[j][:], bias_h[:, (o // NB) % 2, 1:2],
                                       silu[:, j, :], ALU.add, ALU.mult).then_inc(S["h_done"], 1)

            def hidden_lo(k, o):
                j = o % 2
                dve.wait_ge(S["hi_done"], val(k, o, 1, 1))
                V.tensor_tensor(h_lo[j][:], h32[:, j, :], h_hi[j][:].bitcast(F32), ALU.subtract
                                ).then_inc(S["lo_done"], 1)

            def round_(r, first, second, after):
                b = r - 1
                psE, psG = expert_banks(first)

                def attention_lo(b, i):
                    prep(dve, "t_hi1", b, i + 1, NT)
                    dve.wait_ge(S["xmm"], SEED + b * NT + max(i - 1, 0))
                    V.tensor_tensor(a_lo[i % 2][:], psT[i][:], a_hi[i % 2][:].bitcast(F32), ALU.subtract
                                    ).then_inc(S["psT_free"], 1)

                def residual(i):
                    prep(dve, "xmm", b, i + 1, NT)
                    V.scalar_tensor_tensor(row(b, i), psX[i % 2][:], tanh_g[:, 0:1], row(b, i), ALU.mult, ALU.add
                                           ).then_inc(S["psX_free"], 1)

                def ctx_maxima():
                    dve.wait_ge(S["ctx_in"], (r + 1) * 16)
                    V.tensor_reduce(ctx_s[:, 0, :], cv16, AX.X, ALU.max, apply_absolute_value=True
                                    ).then_inc(S["cmax"], 1)

                def ctx_scales():
                    prep(dve, "call", r, 1, 1)
                    V.tensor_scalar(ctx_s[:, 1, :], ctx_s[:, 1, :], W_EPS, None, ALU.max).then_inc(S["cscale"], 1)
                    scales(ctx_s, "cscale", r)

                def ctx_magic():
                    prep(dve, "cv", r, 2, 2)
                    magic(ctx_v, ctx_m, "cm", r)

                def x_scales():
                    prep(dve, "xn1", r, NT, NT)
                    V.tensor_reduce(xs[:, 0, :], xa16, AX.X, ALU.max, apply_absolute_value=True
                                    ).then_inc(S["amax"], 1)
                    prep(dve, "amax", r, 1, 1)
                    V.tensor_scalar(xs[:, 1, :], xs[:, 0, :], ACT_EPS, None, ALU.max).then_inc(S["xsc"], 1)
                    scales(xs, "xsc", r)

                def x_magic():
                    V.tensor_tensor(xa16, xa16, xs[:, 2, :].unsqueeze(2).broadcast_to([P, 16, P]), ALU.mult
                                    ).then_inc(S["xv"], 1)
                    prep(dve, "xv", r, 1, 1)
                    magic(xa_flat, xm_flat, "xmg", r)

                def expert_lo(i):
                    prep(dve, "t_hi2", b, i + 1, NT)
                    cols = bass.ds(b * BT + i * P, P)
                    V.tensor_tensor(xT_lo[:, :, cols], psE[i][:].rearrange("p (c n) -> p c n", c=KC),
                                    xT_hi[:, :, cols].bitcast(F32), ALU.subtract).then_inc(S["psT_free"], 1)

                def split_ctx():
                    prep(dve, "chi", r, 1, 1)
                    V.tensor_tensor(ctx_lo[:].rearrange("p c n -> p (c n)"), ctx_v[:],
                                    ctx_hi[:].rearrange("p c n -> p (c n)").bitcast(F32), ALU.subtract
                                    ).then_inc(S["clo"], 1)

                if not second:
                    ctx_maxima()
                    ctx_scales()
                    x_statistics(0)
                    aggregate(0, True, False)
                    deviation(0)
                    ctx_magic()
                    x_scales()
                    x_magic()
                    x_statistics(1)
                    aggregate(1, True, False)
                    dve.wait_ge(S["gate_hi_done"], 1)
                    V.tensor_tensor(gate_lo[:, :, 0:E], gate_raw[:], gate_hi[:, :, 0:E].bitcast(F32), ALU.subtract
                                    ).then_inc(S["gate_lo_done"], 1)
                    dve.wait_ge(S["tanh_done"], 1)
                    V.tensor_copy(cw[:, :, E:E + 1], tanh_g[:, 1:2].unsqueeze(1).broadcast_to([P, NT, 1])
                                  ).then_inc(S["gate_lo_done"], 1)
                    split_ctx()
                    attention_lo(0, 0)
                    attention_lo(0, 1)
                    deviation(1)
                    return
                if first:
                    ctx_maxima()
                attention_lo(b, 2)
                if first:
                    ctx_scales()
                residual(0)
                attention_lo(b, 3)
                residual(1)
                if after:
                    x_statistics(r + 1)
                if first:
                    ctx_magic()
                residual(2)
                residual(3)
                for i in range(NT):
                    wait_apart(dve, "psX_free", SEED + b * X_USES + i + 1)
                    V.bn_stats(stat[:, 1, i, :], row(b, i)).then_inc(S["st2"], 1)
                aggregate(r + 1, after, second)
                if first:
                    x_scales()
                deviation(r + 1)
                if first:
                    x_magic()
                else:
                    hidden(0, 0)
                for i in range(NT):
                    expert_lo(i)
                if first:
                    split_ctx()
                else:
                    dve.nop().then_inc(S["y_free"], 2)
                    hidden_lo(0, 0)
                    hidden(0, 1)
                    hidden_lo(0, 1)
                    add_out(0, 1, 0)
                    add_out(0, 1, 1)

                def meanwhile():
                    for i in range(2):
                        if first:
                            attention_lo(r, i)
                        else:
                            add_out(0, 1, 2 + i)

                routing(b, psG[1], meanwhile)

            def routing(b, bank, meanwhile):
                prep(dve, "gtp", b, 1, 1)
                ps = bank[:, 0:NT * E].rearrange("p (i e) -> p i e", e=E)
                V.tensor_reduce(g1[:, 0, :], ps, AX.X, ALU.max).then_inc(S["gch"], 1)
                prep(dve, "gch", b, 1, GCH)
                V.tensor_tensor(gt[:, 0], ps, g1[:, 0, :].unsqueeze(2).broadcast_to([P, NT, E]), ALU.subtract
                                ).then_inc(S["gsub"], 1)
                meanwhile()
                prep(dve, "gexp", b, 1, 1)
                V.tensor_reduce(g1[:, 1, :], gt[:, 1], AX.X, ALU.add).then_inc(S["gch"], 1)
                prep(dve, "gch", b, 2, GCH)
                V.reciprocal(g1[:, 2, :], g1[:, 1, :]).then_inc(S["gch"], 1)
                prep(dve, "gch", b, 3, GCH)
                V.tensor_tensor(gt[:, 2], gt[:, 1], g1[:, 2, :].unsqueeze(2).broadcast_to([P, NT, E]), ALU.mult
                                ).then_inc(S["gch"], 1)
                prep(dve, "gch", b, 4, GCH)
                V.tensor_tensor(biased[:, 0, :, 0:E], gt[:, 2], gate_bias[:].unsqueeze(1).broadcast_to([P, NT, E]),
                                ALU.add).then_inc(S["gch"], 1)
                wait_apart(dve, "gch", b * GCH + 5)
                for i in range(NT):
                    V.max(top8[:, i, :], biased[:, 0, i, 0:E]).then_inc(S["gch"], 1)
                prep(dve, "gch", b, 5 + NT, GCH)
                V.memset(top8[:, :, TOP_K:8], ABSENT).then_inc(S["gch"], 1)
                wait_apart(dve, "gch", b * GCH + 6 + NT)
                for i in range(NT):
                    V.match_replace(biased[:, 1, i, :], top8[:, i, :], biased[:, 0, i, :], TAKEN
                                    ).then_inc(S["gch"], 1)
                prep(dve, "gch", b, 6 + 2 * NT, GCH)
                V.scalar_tensor_tensor(gt[:, 0], biased[:, 1, :, 0:E], TAKEN, gt[:, 2], ALU.is_equal, ALU.mult
                                       ).then_inc(S["gch"], 1)
                prep(dve, "gch", b, 7 + 2 * NT, GCH)
                dve.wait_ge(S["cwt_free"], SEED + b)
                V.tensor_scalar(cw[:, :, 0:E], gt[:, 0], tanh_g[:, 1:2], None, ALU.mult).then_inc(S["cwd"], 1)

            rounds(dve, round_)

            def step(k, o):
                add_out(k, o, 0)
                add_out(k, o, 1)
                hidden(k, o)
                add_out(k, o, 2)
                hidden_lo(k, o)
                add_out(k, o, 3)

            step(0, EARLY - 1)
            with dve.Fori(0, LOOPS) as k:
                for o in range(EARLY, BODY + EARLY):
                    step(k, o)
            for o in range(BODY * LOOPS + EARLY, STEPS):
                step(0, o)
            for i in range(NT):
                add_out(0, STEPS, i)

        @block.tensor
        def _(pe):
            def three(out, a_hi, a_lo, b_hi, b_lo, start, stop):
                nc.tensor.matmul(out, a_hi, b_hi, start=start, stop=False)
                nc.tensor.matmul(out, a_hi, b_lo, start=False, stop=False)
                return nc.tensor.matmul(out, a_lo, b_hi, start=False, stop=stop)

            pe.wait_ge(S["gates_in"], 16 * 5)

            def up(k, o, which):
                j, w, b = o % 2, (o // NB) % 2, o % NB
                out = (psA, psB)[which][j]
                if o > 1:
                    pe.wait_ge(S["h_done" if which else "silu_done"], val(k, o, 1, -1))
                for c in range(KC):
                    cols = slice(which * D + c * P, which * D + (c + 1) * P)
                    tok = slice(b * BT, (b + 1) * BT)
                    last = three(out[:], w_hi[w][:, cols], w_lo[w][:, cols], xT_hi[:, c, tok], xT_lo[:, c, tok],
                                 c == 0, c == KC - 1)
                last.then_inc(S["b_ready" if which else "a_ready"], 1)

            def down(k, o, i):
                j, w = (o - 1) % 2, ((o - 1) // NB) % 2
                pe.wait_ge(S["y_free"], val(k, o, NT, -NT + i + 1))
                tok = slice(i * P, (i + 1) * P)
                three(psY[i % 2][:], h_hi[j][:, tok], h_lo[j][:, tok], w_hi[w][:, 2 * D:3 * D],
                      w_lo[w][:, 2 * D:3 * D], True, True).then_inc(S["y_ready"], 1)

            def round_(r, first, second, after):
                b = r - 1
                psE, psG = expert_banks(first)

                def transposes(bank, i, src, signal):
                    for c in range(KC):
                        last = nc.tensor.transpose(bank[:, c * P:(c + 1) * P],
                                                   src[:, i, c * P:(c + 1) * P], ident[:])
                    last.then_inc(S[signal], 1)

                def attention_T(i):
                    pe.wait_ge(S["psT_free"], SEED + r * T_USES)
                    prep(pe, "xdq", r, i + 1, NT)
                    transposes(psT[i], i, xa, "tp1")

                def attend(b, i):
                    prep(pe, "psT_free", b, i + 1, T_USES)
                    prep(pe, "clo", b, 1, 1)
                    pe.wait_ge(S["psX_free"], SEED + b * X_USES + max(i - 1, 0))
                    for c in range(KC):
                        cols = slice(c * P, (c + 1) * P)
                        last = three(psX[i % 2][:], a_hi[i % 2][:, cols], a_lo[i % 2][:, cols], ctx_hi[:, c, :],
                                     ctx_lo[:, c, :], c == 0, c == KC - 1)
                    last.then_inc(S["xmm"], 1)

                if second:
                    for i in range(1, NT):
                        attend(b, i)
                    if not first:
                        pe.wait_ge(S["w_lo_done"], 1)
                        up(0, 0, 0)
                        up(0, 0, 1)
                        up(0, 1, 0)
                    pe.wait_ge(S["psX_free"], SEED + b * X_USES + NT)
                    for i in range(NT):
                        prep(pe, "xn2", b, i + 1, NT)
                        if i == 0:
                            pe.wait_ge(S["cwt_free"], SEED + b)
                        transposes(psE[i], i, xb, "tp2")
                    if not first:
                        up(0, 1, 1)
                    pe.wait_ge(S["psT_free"], SEED + b * T_USES + 2 * NT)
                    cols = bass.ds(b * BT, BT)
                    for c in range(KC):
                        last = three(psG[0][:], gate_hi[:, c, :], gate_lo[:, c, :], xT_hi[:, c, cols],
                                     xT_lo[:, c, cols], c == 0, c == KC - 1)
                    last.then_inc(S["gmm"], 1)
                if first:
                    attention_T(0)
                    attention_T(1)
                else:
                    pe.wait_ge(S["lo_done"], 1)
                    down(0, 1, 0)
                    down(0, 1, 1)
                if second:
                    wait_apart(pe, "psX_free", SEED + b * X_USES + NT + 1)
                    for i in range(NT):
                        last = nc.tensor.transpose(psG[1][:, i * E:(i + 1) * E], score[:, i * P:(i + 1) * P],
                                                   ident[0:E, 0:E])
                    last.then_inc(S["gtp"], 1)
                if first:
                    if not second:
                        pe.wait_ge(S["gate_lo_done"], 2)
                    attend(r, 0)
                    attention_T(2)
                    attention_T(3)
                else:
                    down(0, 1, 2)
                    down(0, 1, 3)
                    up(0, 2, 0)
                    pe.wait_ge(S["lo_done"], 2)
                    down(0, 2, 0)
                    down(0, 2, 1)
                    up(0, 2, 1)
                if second:
                    prep(pe, "cwd", b, 1, 1)
                    for i in range(NT):
                        last = nc.tensor.transpose(psT[0][0:E + 1, i * P:(i + 1) * P], cw[:, i, :], ident[:])
                    last.then_inc(S["cwtp"], 1)

            rounds(pe, round_)

            def step(k, o):
                if o % NB == 0:
                    pe.wait_ge(S["w_lo_done"], k * 2 + o // NB + 1)
                up(k, o, 0)
                pe.wait_ge(S["lo_done"], val(k, o))
                down(k, o, 0)
                down(k, o, 1)
                up(k, o, 1)
                down(k, o, 2)
                down(k, o, 3)

            down(0, EARLY - 1, 2)
            down(0, EARLY - 1, 3)
            with pe.Fori(0, LOOPS) as k:
                for o in range(EARLY, BODY + EARLY):
                    step(k, o)
            for o in range(BODY * LOOPS + EARLY, STEPS):
                step(0, o)
            pe.wait_ge(S["lo_done"], STEPS)
            for i in range(NT):
                down(0, STEPS, i)


_OUT = (NB, BT, D)


def kernel(x, ctx_2048, g_xattn, g_ffn, L0_ffn_gate_w, L0_ffn_gate_b, L0_ffn_w1, L0_ffn_b1, L0_ffn_w2, L0_ffn_b2,
           L0_ffn_w3, L0_ffn_b3, L0_ffn_ws1, L0_ffn_bs1, L0_ffn_ws2, L0_ffn_bs2, L0_ffn_ws3, L0_ffn_bs3):
    import numpy as np
    import concourse.bacc as bacc
    from concourse.bass_utils import run_bass_kernel_spmd

    def rows(experts, shared, spare=0.0):
        a = np.concatenate([np.asarray(experts).reshape(E * H, -1), np.asarray(shared).reshape(HS, -1)])
        return np.concatenate([a, np.full((CH * P - HID, a.shape[1]), spare, a.dtype)])

    def up(w):
        return w.reshape(CH, P, KC, P).transpose(0, 3, 2, 1).reshape(CH, P, D)

    w1, w3 = rows(L0_ffn_w1, L0_ffn_ws1), rows(L0_ffn_w3, L0_ffn_ws3)
    w2 = rows(np.asarray(L0_ffn_w2).transpose(0, 2, 1), np.asarray(L0_ffn_ws2).T).reshape(CH, P, D)
    w2[CH - 1, BIAS_ROW:BIAS_ROW + E] = L0_ffn_b2
    w2[CH - 1, BIAS_ROW + E] = L0_ffn_bs2
    b1 = rows(L0_ffn_b1, L0_ffn_bs1, SPARE_B1).reshape(CH, P, 1)
    b3 = rows(L0_ffn_b3, L0_ffn_bs3, 1.0 / SPARE_B1).reshape(CH, P, 1)
    arrays = {
        "x": np.ascontiguousarray(np.asarray(x).reshape(T, D)),
        "ctxT": np.ascontiguousarray(np.asarray(ctx_2048).transpose(0, 2, 1)),
        "g_xattn": np.ascontiguousarray(g_xattn),
        "g_ffn": np.ascontiguousarray(g_ffn),
        "gate_wT": np.ascontiguousarray(np.asarray(L0_ffn_gate_w).T),
        "gate_b": np.ascontiguousarray(L0_ffn_gate_b),
        "w_all": np.ascontiguousarray(np.concatenate([up(w1), up(w3), w2, b1, b3], axis=2)),
        "ident": np.eye(P, dtype=np.float32),
    }
    nc = bacc.Bacc("TRN2", target_bir_lowering=False, num_devices=1)
    t = {n: nc.dram_tensor(n, a.shape, mybir.dt.from_np(a.dtype), kind="ExternalInput").ap()
         for n, a in arrays.items()}
    t["out"] = nc.dram_tensor("out", (T, D), F32, kind="ExternalOutput").ap()
    build(nc, t)
    r = run_bass_kernel_spmd(nc, [arrays], core_ids=[0])
    return r.results[0]["out"].reshape(_OUT)
```
